# Optimizing a Trainium2 kernel written in Bass

```python
import numpy as np
import jax
import jax.numpy as jnp

def _softmax(x, axis=-1):
    return jax.nn.softmax(x, axis=axis)

def _gelu(x):
    return jax.nn.gelu(x, approximate=True)

def _silu(x):
    return jax.nn.silu(x)

def _sigmoid(x):
    return jax.nn.sigmoid(x)

def _layernorm(x, axis=-1, eps=1e-05):
    m = jnp.mean(x, axis=axis, keepdims=True)
    v = jnp.var(x, axis=axis, keepdims=True)
    return (x - m) / jnp.sqrt(v + eps)

def _scatter_add(tgt, idx, src, axis=0):
    return tgt.at[idx].add(src)

def _segment_sum(src, seg, n):
    return jax.ops.segment_sum(src, seg, n)
kernel_name = 'mk_gnn_preln_d1_gnn_r8_954763'

def setup_inputs(seed: int=0):
    np.random.seed(seed)
    _w = jnp.asarray

    def _rec_inputs():
        import jax
        import jax.numpy as jnp
        _gk = jax.random.key(seed)
        x = -0.000202 + 1 * jax.random.normal(jax.random.fold_in(_gk, 1), (12500, 128), jnp.float32)
        src = jax.random.randint(jax.random.fold_in(_gk, 2), (400000,), 0, 12500, jnp.int32)
        dst = jax.random.randint(jax.random.fold_in(_gk, 3), (400000,), 0, 12500, jnp.int32)
        _o = jnp.argsort(dst, stable=True)
        src = src[_o]
        dst = dst[_o]
        return (x, src, dst)
    x, src, dst = _rec_inputs()

    def _L0_gnn_setup():
        import jax, jax.numpy as jnp
        import numpy as np
        N_NODES = 6250
        N_EDGES = 100000
        DIM = 128
        BN_EPS = 1e-05
        key = jax.random.key(seed)
        ks = jax.random.split(key, 12)
        d = DIM
        s = 1.0 / np.sqrt(d)
        x = jax.random.normal(ks[0], (N_NODES, d), dtype=jnp.float32)
        edge_index = jax.random.randint(ks[1], (2, N_EDGES), 0, N_NODES, dtype=jnp.int64)
        W_msg = jax.random.uniform(ks[2], (d, d), jnp.float32, -s, s)
        b_msg = jax.random.uniform(ks[3], (d,), jnp.float32, -s, s)
        sa = 1.0 / np.sqrt(2 * d)
        W_att = jax.random.uniform(ks[4], (2 * d, 1), jnp.float32, -sa, sa)
        b_att = jax.random.uniform(ks[5], (1,), jnp.float32, -sa, sa)
        W_ih = jax.random.uniform(ks[6], (3 * d, d), jnp.float32, -s, s)
        b_ih = jax.random.uniform(ks[7], (3 * d,), jnp.float32, -s, s)
        W_hh = jax.random.uniform(ks[8], (3 * d, d), jnp.float32, -s, s)
        b_hh = jax.random.uniform(ks[9], (3 * d,), jnp.float32, -s, s)
        gamma = jnp.ones((d,), jnp.float32)
        beta = jnp.zeros((d,), jnp.float32)
        return {'x': x, 'edge_index': edge_index, 'W_msg': W_msg, 'b_msg': b_msg, 'W_att': W_att, 'b_att': b_att, 'W_ih': W_ih, 'b_ih': b_ih, 'W_hh': W_hh, 'b_hh': b_hh, 'gamma': gamma, 'beta': beta}
    _L0_gnn_all = _L0_gnn_setup()
    _L0_gnn_in = {k: v for k, v in _L0_gnn_all.items() if k in ('W_msg', 'b_msg', 'W_att', 'b_att', 'W_ih', 'b_ih', 'W_hh', 'b_hh', 'gamma', 'beta')}
    del _L0_gnn_all
    return {'x': x, 'src': src, 'dst': dst, 'L0_gnn_W_msg': _L0_gnn_in['W_msg'], 'L0_gnn_b_msg': _L0_gnn_in['b_msg'], 'L0_gnn_W_att': _L0_gnn_in['W_att'], 'L0_gnn_b_att': _L0_gnn_in['b_att'], 'L0_gnn_W_ih': _L0_gnn_in['W_ih'], 'L0_gnn_b_ih': _L0_gnn_in['b_ih'], 'L0_gnn_W_hh': _L0_gnn_in['W_hh'], 'L0_gnn_b_hh': _L0_gnn_in['b_hh'], 'L0_gnn_gamma': _L0_gnn_in['gamma'], 'L0_gnn_beta': _L0_gnn_in['beta']}

def reference(x, src, dst, L0_gnn_W_msg, L0_gnn_b_msg, L0_gnn_W_att, L0_gnn_b_att, L0_gnn_W_ih, L0_gnn_b_ih, L0_gnn_W_hh, L0_gnn_b_hh, L0_gnn_gamma, L0_gnn_beta):
    import jax
    import jax.numpy as jnp

    def _L0_gnn_ref(x, edge_index, W_msg, b_msg, W_att, b_att, W_ih, b_ih, W_hh, b_hh, gamma, beta):
        import jax, jax.numpy as jnp
        import numpy as np
        N_NODES = 6250
        N_EDGES = 100000
        DIM = 128
        BN_EPS = 1e-05
        num_nodes, d = x.shape
        src = edge_index[0]
        dst = edge_index[1]
        xs = x[src]
        xd = x[dst]
        att = jax.nn.sigmoid(xs @ W_att[:d] + xd @ W_att[d:] + b_att)
        messages = (xs @ W_msg + b_msg) * att
        aggregated = jax.ops.segment_sum(messages, dst, num_segments=num_nodes)
        gi = aggregated @ W_ih.T + b_ih
        gh = x @ W_hh.T + b_hh
        i_r, i_z, i_n = jnp.split(gi, 3, axis=1)
        h_r, h_z, h_n = jnp.split(gh, 3, axis=1)
        r = jax.nn.sigmoid(i_r + h_r)
        z = jax.nn.sigmoid(i_z + h_z)
        n = jnp.tanh(i_n + r * h_n)
        h_new = (1.0 - z) * n + z * x
        mean = jnp.mean(h_new, axis=0)
        var = jnp.var(h_new, axis=0)
        return gamma * (h_new - mean) * jax.lax.rsqrt(var + BN_EPS) + beta
    edge_index = jnp.stack([src, dst])
    h = jnp.maximum(_layernorm(x, axis=-1), 0.0)
    x = x + _L0_gnn_ref(h, edge_index, L0_gnn_W_msg, L0_gnn_b_msg, L0_gnn_W_att, L0_gnn_b_att, L0_gnn_W_ih, L0_gnn_b_ih, L0_gnn_W_hh, L0_gnn_b_hh, L0_gnn_gamma, L0_gnn_beta)
    return x

_drawn_inputs = setup_inputs


def setup_inputs(seed=0):
    import zlib

    import numpy as np

    out = dict(_drawn_inputs(seed))
    spreads = {'L0_gnn_gamma': (1.0, 0.2), 'L0_gnn_beta': (0.0, 0.1)}
    factors = {'L0_gnn_b_ih': 4.688, 'L0_gnn_b_hh': 4.889}
    for name, (base, spread) in spreads.items():
        noise = np.random.default_rng([zlib.crc32(name.encode()), seed]).standard_normal(out[name].shape)
        drawn = base * np.exp(spread * noise) if base else spread * noise
        out[name] = jnp.asarray(drawn.astype(out[name].dtype))
    for name, factor in factors.items():
        out[name] = (out[name] * factor).astype(out[name].dtype)
    return out
```

```python
from contextlib import ExitStack

import concourse.bass as bass
from concourse import mybir

F32 = mybir.dt.float32
I32 = mybir.dt.int32
U32 = mybir.dt.uint32
ALU = mybir.AluOpType
ACT = mybir.ActivationFunctionType
AX_X = mybir.AxisListType.X

P = 128
SLOTS = 8
CHUNK = 512
TILES_PER_CHUNK = CHUNK // P
EPS = 1e-5


def up(n, m):
    return -(-n // m) * m


def gnn_program(nc, x, src, dst, W_msg, b_msg, W_att, b_att, W_ih, b_ih, W_hh, b_hh, gamma, beta, out):
    NODES, D = x.shape
    EDGES = src.shape[0]
    assert D == P and EDGES % P == 0
    TILES = EDGES // P
    ROWS = next(r for r in range(P, 0, -1) if TILES % r == 0)
    COLS = TILES // ROWS
    STEPS = up(TILES + (NODES - 1) // P, SLOTS)
    EXTRA = STEPS - TILES
    assert EXTRA <= P
    TURNS = STEPS // SLOTS
    PAD = NODES + P
    ROW = D + 1
    CHUNKS = -(-NODES // CHUNK)
    LAST = NODES - (CHUNKS - 1) * CHUNK
    FULL_TURNS = (CHUNKS - 1) // 2
    assert (CHUNKS - 1) % 2 == 0

    table = nc.dram_tensor("node_table", (NODES, ROW), F32, kind="Internal").ap()
    hT_dram = nc.dram_tensor("hT_spill", (P, NODES), F32, kind="Internal").ap()
    base_dram = nc.dram_tensor("window_starts", (1, STEPS), I32, kind="Internal").ap()

    with ExitStack() as ctx:
        def sb(name, shape, dt=F32):
            return ctx.enter_context(nc.sbuf_tensor(name, shape, dt))

        def sem(name):
            return ctx.enter_context(nc.semaphore(name))

        def sems(name, n):
            return [sem(f"{name}{i}") for i in range(n)]

        ident = sb("ident", [P, P])
        ones = sb("ones", [P, P])
        before = sb("before", [P, P])
        lane = sb("lane", [P, P])
        lane_p = sb("lane_p", [P, 1])
        eps = sb("eps", [P, 1])
        w_table = sb("w_table", [P, ROW])
        w_att_dst = sb("w_att_dst", [P, 1])
        w_att_dst_wide = sb("w_att_dst_wide", [P, P])
        b_table = sb("b_table", [P, ROW])
        b_att_all = sb("b_att_all", [P, 1])
        gates_nat = sb("gates_nat", [P, 6, P])
        gates = sb("gates", [P, 6, P])
        b_gates = sb("b_gates", [P, 6])
        b_rz = sb("b_rz", [P, 2])
        gamma_c = sb("gamma_c", [P, 1])
        beta_c = sb("beta_c", [P, 1])

        src_cols = sb("src_cols", [P, STEPS + SLOTS])
        dst_cols = sb("dst_cols", [P, STEPS])
        starts = sb("starts", [1, STEPS], I32)
        agg = sb("agg", [P, PAD])
        region = sb("region", [P, max(4 * COLS * P, PAD, CHUNKS * CHUNK)])
        dst_score = region[:, 0:PAD]
        x_again = region[:, 0:CHUNKS * CHUNK].rearrange("p (t d) -> p t d", d=D)
        E = COLS * P
        dst_int = agg[0:ROWS, 0:E].bitcast(I32)
        src_int = agg[0:ROWS, E:2 * E].bitcast(I32)
        dst_f = agg[0:ROWS, 2 * E:3 * E]
        src_f = region[0:ROWS, 0:E]
        dst_rel = region[0:ROWS, E:2 * E]
        within = region[0:ROWS, 2 * E:2 * E + EXTRA * COLS].rearrange("p (k c) -> p k c", c=COLS)
        within_x = region[0:ROWS, 3 * E:3 * E + EXTRA * COLS].rearrange("p (k c) -> p k c", c=COLS)

        first_f = sb("first_f", [ROWS, COLS])
        span_f = sb("span_f", [ROWS, COLS])
        span_i = sb("span_i", [ROWS, COLS], I32)
        more_i = sb("more_i", [ROWS, COLS], I32)
        more_f = sb("more_f", [ROWS, COLS])
        more_sum = sb("more_sum", [ROWS, COLS])
        first_i = sb("first_i", [ROWS, COLS], I32)
        row_before = sb("row_before", [ROWS, 1])
        count = sb("count", [ROWS, 2, EXTRA])
        ex = sb("ex", [P, 8])
        ex_idx = sb("ex_idx", [P, 1], U32)
        ex_start = sb("ex_start", [P, 1], I32)
        ex_int = sb("ex_int", [P, 2, P], I32)
        ex_f = sb("ex_f", [P, 2, P])
        ex_rel = sb("ex_rel", [P, P])

        xbuf = sb("xbuf", [P, 2, TILES_PER_CHUNK, P])
        zbuf = sb("zbuf", [P, 2, TILES_PER_CHUNK, P])
        hbuf = sb("hbuf", [P, 2, CHUNK])
        rows_out = sb("rows_out", [P, 2, TILES_PER_CHUNK, ROW])
        stats = sb("stats", [P, 2, TILES_PER_CHUNK, 6])
        mv = sb("mv", [P, 2, TILES_PER_CHUNK, 2])
        std = sb("std", [P, 2, TILES_PER_CHUNK])
        rstd = sb("rstd", [P, 2, TILES_PER_CHUNK])
        r_sb = xbuf[:, :, :, :].rearrange("p b t d -> p b (t d)")
        z_sb = zbuf[:, :, :, :].rearrange("p b t d -> p b (t d)")
        n_sb = rows_out[:, :, :, :].rearrange("p b t d -> p b (t d)")
        t_sb = sb("t_sb", [P, 2, CHUNK])
        bn_all = sb("bn_all", [P, CHUNKS, 6])
        bn_mv = sb("bn_mv", [P, 2])
        bn = sb("bn", [P, 4])

        idx_ring = sb("idx_ring", [P, SLOTS], U32)
        row_ring = sb("row_ring", [P, SLOTS, ROW])
        gate_ring = sb("gate_ring", [P, SLOTS, P])
        mask_ring = sb("mask_ring", [P, SLOTS, P])

        ps = ctx.enter_context(nc.psum_tensor("ps", [P, 8, 512], F32))

        consts_loaded = sem("consts_loaded")
        edges_loaded = sem("edges_loaded")
        consts_made = sem("consts_made")
        wide_made = sem("wide_made")
        dve_line = sem("dve_line")
        prefix_done = sem("prefix_done")
        counts_made = sem("counts_made")
        counts_summed = sem("counts_summed")
        ex_idx_made = sem("ex_idx_made")
        ex_gathered = sem("ex_gathered")
        rel_made = sem("rel_made")
        ex_made = sem("ex_made")
        starts_made = sem("starts_made")
        starts_in_dram = sem("starts_in_dram")
        starts_loaded = sem("starts_loaded")
        edge_turned = sem("edge_turned")
        edge_kept = sem("edge_kept")
        gates_turned = sem("gates_turned")
        gates_kept = sem("gates_kept")
        agg_zeroed = sem("agg_zeroed")

        x_loaded = sems("x_loaded", 2)
        stats_done = sems("stats_done", 2)
        mv_done = sems("mv_done", 2)
        std_done = sems("std_done", 2)
        rstd_done = sems("rstd_done", 2)
        z_done = sems("z_done", 2)
        z_turned = sems("z_turned", 2)
        h_done = sems("h_done", 2)
        dense_done = sems("dense_done", 2)
        rows_done = sems("rows_done", 2)
        score_done = sems("score_done", 2)
        table_stored = sems("table_stored", 2)
        h_stored = sems("h_stored", 2)

        idx_first = sem("idx_first")
        idx_ready = sems("idx_ready", SLOTS)
        gathered = sems("gathered", SLOTS)
        gate_ready = sems("gate_ready", SLOTS)
        mask_ready = sems("mask_ready", SLOTS)
        summed = sems("summed", SLOTS)
        added = sems("added", SLOTS)

        h_loaded = sems("h_loaded", 2)
        x_back = sem("x_back")
        gru_done = sems("gru_done", 2)
        r_done = sems("r_done", 2)
        zg_done = sems("zg_done", 2)
        t_done = sems("t_done", 2)
        u_done = sems("u_done", 2)
        n_done = sems("n_done", 2)
        d_done = sems("d_done", 2)
        e_done = sems("e_done", 2)
        new_done = sems("new_done", 2)
        bn_done = sems("bn_done", 2)
        bn_line = sem("bn_line")
        bn_std = sem("bn_std")
        y_done = sems("y_done", 2)
        y_turned = sems("y_turned", 2)
        o_done = sems("o_done", 2)
        o_stored = sems("o_stored", 2)

        edge_groups = [list(range(g, min(g + 4, COLS))) for g in range(0, COLS, 4)]
        N_GROUPS = 2 * len(edge_groups) + 1

        def tiles_of(width):
            return [(j, min(P, width - j * P)) for j in range(-(-width // P))]


        block = ctx.enter_context(nc.Block())

        @block.sync
        def _(sp):
            sp.dma_start(dst_int, dst.rearrange("(p e) -> p e", e=E)).then_inc(edges_loaded, 16)
            sp.dma_start(src_int, src.rearrange("(p e) -> p e", e=E)).then_inc(edges_loaded, 16)

            def load_x(turn, b, start, width):
                for j, n in ([(None, width)] if width == CHUNK else tiles_of(width)):
                    if j is None:
                        sp.dma_start(xbuf[:, b, :, :], x[bass.ds(start, CHUNK), :].rearrange("(t p) d -> p t d", p=P)
                                     ).then_inc(x_loaded[b], 16)
                    else:
                        sp.dma_start(xbuf[0:n, b, j, :], x[start + j * P:start + j * P + n, :]).then_inc(x_loaded[b], 16)

            def store(turn, b, start, width):
                sp.wait_ge(h_done[b], turn + 1)
                sp.dma_start(hT_dram[:, bass.ds(start, width)], hbuf[:, b, 0:width]).then_inc(h_stored[b], 16)
                sp.wait_ge(rows_done[b], turn + 1)
                if width == CHUNK:
                    sp.dma_start(table[bass.ds(start, CHUNK), :].rearrange("(t p) d -> p t d", p=P),
                                 rows_out[:, b, :, :]).then_inc(table_stored[b], 16)
                else:
                    for j, n in tiles_of(width):
                        sp.dma_start(table[start + j * P:start + j * P + n, :],
                                     rows_out[0:n, b, j, :]).then_inc(table_stored[b], 16)

            load_x(0, 0, 0, CHUNK)
            load_x(0, 1, CHUNK, CHUNK)
            sp.dma_start(w_table[:, 0:D], W_msg).then_inc(consts_loaded, 16)
            sp.dma_start(w_table[:, D:ROW], W_att[0:D, :]).then_inc(consts_loaded, 16)
            sp.dma_start(w_att_dst[:, :], W_att[D:2 * D, :]).then_inc(consts_loaded, 16)
            sp.dma_start(b_table[:, 0:D], b_msg.rearrange("(o d) -> o d", o=1).broadcast_to((P, D))
                         ).then_inc(consts_loaded, 16)
            sp.dma_start(b_att_all[:, :], b_att.rearrange("(o d) -> o d", o=1).broadcast_to((P, 1))
                         ).then_inc(consts_loaded, 16)
            sp.dma_start(gates_nat[:, 0:3, :], W_ih.rearrange("(g o) d -> o g d", o=P)).then_inc(consts_loaded, 16)
            sp.dma_start(gates_nat[:, 3:6, :], W_hh.rearrange("(g o) d -> o g d", o=P)).then_inc(consts_loaded, 16)
            for g in range(3):
                sp.dma_start(b_gates[:, g:g + 1], b_ih[g * P:(g + 1) * P].rearrange("(d o) -> d o", o=1)
                             ).then_inc(consts_loaded, 16)
                sp.dma_start(b_gates[:, 3 + g:4 + g], b_hh[g * P:(g + 1) * P].rearrange("(d o) -> d o", o=1)
                             ).then_inc(consts_loaded, 16)
            sp.dma_start(gamma_c[:, :], gamma.rearrange("(d o) -> d o", o=1)).then_inc(consts_loaded, 16)
            sp.dma_start(beta_c[:, :], beta.rearrange("(d o) -> d o", o=1)).then_inc(consts_loaded, 16)

            sp.wait_ge(starts_made, 2)
            sp.dma_start(base_dram[:, 0:TILES].rearrange("o (p c) -> (o p) c", c=COLS), first_i[:, :]
                         ).then_inc(starts_in_dram, 16)
            sp.dma_start(base_dram[:, TILES:STEPS].rearrange("o k -> k o"), ex_start[0:EXTRA, :]
                         ).then_inc(starts_in_dram, 16)
            sp.wait_ge(starts_in_dram, 32)
            sp.dma_start(starts[:, :], base_dram).then_inc(starts_loaded, 16)

            for b in range(2):
                store(0, b, b * CHUNK, CHUNK)
                sp.wait_ge(z_done[b], 1)
                load_x(1, b, (2 + b) * CHUNK, CHUNK)
            with sp.Fori(1, FULL_TURNS - 1) as turn:
                for b in range(2):
                    store(turn, b, (2 * turn + b) * CHUNK, CHUNK)
                    sp.wait_ge(z_done[b], turn + 1)
                    load_x(turn + 1, b, (2 * turn + 2 + b) * CHUNK, CHUNK)
            for b in range(2):
                c = CHUNKS - 3 + b
                store(FULL_TURNS - 1, b, c * CHUNK, CHUNK)
                if b == 0:
                    sp.wait_ge(z_done[b], FULL_TURNS)
                    load_x(FULL_TURNS, b, (CHUNKS - 1) * CHUNK, LAST)
            store(FULL_TURNS, 0, (CHUNKS - 1) * CHUNK, LAST)

            def load_h(b, start, width):
                sp.dma_start(hbuf[:, b, 0:width], hT_dram[:, bass.ds(start, width)]).then_inc(h_loaded[b], 16)

            sp.wait_ge(h_stored[0], 16 * (FULL_TURNS + 1))
            sp.wait_ge(h_stored[1], 16 * FULL_TURNS)
            load_h(0, 0, CHUNK)
            load_h(1, CHUNK, CHUNK)
            sp.wait_ge(gate_ready[SLOTS - 1], TURNS)
            whole = NODES // P
            sp.dma_start(x_again[:, 0:whole, :], x[0:whole * P, :].rearrange("(t p) d -> p t d", p=P)
                         ).then_inc(x_back, 16)
            sp.dma_start(x_again[0:NODES - whole * P, whole, :], x[whole * P:NODES, :]).then_inc(x_back, 16)
            with sp.Fori(1, FULL_TURNS) as turn:
                for b in range(2):
                    sp.wait_ge(new_done[b], turn)
                    load_h(b, (2 * turn + b) * CHUNK, CHUNK)
            sp.wait_ge(new_done[0], FULL_TURNS)
            load_h(0, (CHUNKS - 1) * CHUNK, LAST)

            def store_out(turn, b, start, width):
                sp.wait_ge(o_done[b], turn + 1)
                if width == CHUNK:
                    sp.dma_start(out[bass.ds(start, CHUNK), :].rearrange("(t p) d -> p t d", p=P),
                                 xbuf[:, b, :, :]).then_inc(o_stored[b], 16)
                else:
                    for j, n in tiles_of(width):
                        sp.dma_start(out[start + j * P:start + j * P + n, :], xbuf[0:n, b, j, :]
                                     ).then_inc(o_stored[b], 16)

            with sp.Fori(0, FULL_TURNS) as turn:
                for b in range(2):
                    store_out(turn, b, (2 * turn + b) * CHUNK, CHUNK)
            store_out(FULL_TURNS, 0, (CHUNKS - 1) * CHUNK, LAST)
            sp.wait_ge(o_stored[0], 16 * (FULL_TURNS + len(tiles_of(LAST))))
            sp.wait_ge(o_stored[1], 16 * FULL_TURNS)

        @block.gpsimd
        def _(pool):
            nc.gpsimd.memset(ones[:, :], 1.0).then_inc(consts_made, 1)
            nc.gpsimd.memset(eps[:, :], EPS).then_inc(consts_made, 1)
            nc.gpsimd.memset(b_table[:, D:ROW], 0.0).then_inc(consts_made, 1)
            nc.gpsimd.memset(src_cols[:, STEPS:STEPS + SLOTS], 0.0).then_inc(consts_made, 1)
            nc.gpsimd.iota(lane[:, :], [[1, P]], base=0, channel_multiplier=0,
                           allow_small_or_imprecise_dtypes=True).then_inc(consts_made, 1)
            nc.gpsimd.iota(lane_p[:, :], [[0, 1]], base=0, channel_multiplier=1,
                           allow_small_or_imprecise_dtypes=True).then_inc(consts_made, 1)
            pool.wait_ge(consts_made, 6)
            nc.gpsimd.affine_select(out=ident[:, :], in_=ones[:, :], compare_op=ALU.is_equal, fill=0.0, base=0,
                                    pattern=[[1, P]], channel_multiplier=-1).then_inc(consts_made, 1)
            nc.gpsimd.affine_select(out=before[:, :], in_=ones[:, :], compare_op=ALU.is_gt, fill=0.0, base=0,
                                    pattern=[[1, P]], channel_multiplier=-1).then_inc(consts_made, 1)

            pool.wait_ge(ex_idx_made, 1)
            for i, edges in enumerate((src, dst)):
                nc.gpsimd.indirect_dma_start(
                    ex_int[0:EXTRA, i, :], None, edges.rearrange("(t e) -> t e", e=P),
                    bass.IndirectOffsetOnAxis(ap=ex_idx[0:EXTRA, :], axis=0)).then_inc(ex_gathered, 16)

            pool.wait_ge(edge_turned, N_GROUPS)
            nc.gpsimd.memset(agg[:, :], 0.0).then_inc(agg_zeroed, 1)

            pool.wait_ge(table_stored[0], 16 * (FULL_TURNS + len(tiles_of(LAST))))
            pool.wait_ge(table_stored[1], 16 * FULL_TURNS)

            def gather(j):
                nc.gpsimd.indirect_dma_start(
                    row_ring[:, j, :], None, table,
                    bass.IndirectOffsetOnAxis(ap=idx_ring[:, j:j + 1], axis=0)).then_inc(gathered[j], 16)

            for j in range(SLOTS):
                pool.wait_ge(idx_first, j + 1)
                gather(j)
            with pool.Fori(1, TURNS) as turn:
                for j in range(SLOTS):
                    pool.wait_ge(table_stored[1], 16 * FULL_TURNS)
                    pool.wait_ge(idx_ready[j], turn)
                    pool.wait_ge(summed[j], turn)
                    gather(j)

        @block.scalar
        def _(act):
            def std_step(turn, b, width):
                act.wait_ge(mv_done[b], turn + 1)
                nc.scalar.activation(std[:, b, 0:len(tiles_of(width))], mv[:, b, 0:len(tiles_of(width)), 1],
                                     ACT.Sqrt, bias=eps[:, 0:1]).then_inc(std_done[b], 1)

            def relu_step(turn, b, width, first):
                act.wait_ge(z_turned[b], turn + 1)
                if not first:
                    act.wait_ge(h_stored[b], 16 * turn)
                    act.wait_ge(dense_done[b], turn)
                nc.scalar.activation(hbuf[:, b, 0:width], ps[:, b, 0:width], ACT.Relu).then_inc(h_done[b], 1)

            def score_step(turn, b, start, width):
                act.wait_ge(dense_done[b], turn + 1)
                nc.scalar.activation(dst_score[:, bass.ds(start, width)], ps[:, 2 + b, 0:width], ACT.Identity,
                                     bias=b_att_all[:, 0:1]).then_inc(score_done[b], 1)

            act.wait_ge(consts_made, 8)
            act.wait_ge(consts_loaded, 16 * 15)
            std_step(0, 0, CHUNK)
            relu_step(0, 0, CHUNK, True)
            act.wait_ge(edge_turned, N_GROUPS)
            std_step(0, 1, CHUNK)
            relu_step(0, 1, CHUNK, True)
            score_step(0, 0, 0, CHUNK)
            with act.Fori(1, FULL_TURNS) as turn:
                for b in range(2):
                    std_step(turn, b, CHUNK)
                    relu_step(turn, b, CHUNK, False)
                    score_step(turn - 1 + b, 1 - b, (2 * turn + b - 1) * CHUNK, CHUNK)
            std_step(FULL_TURNS, 0, LAST)
            relu_step(FULL_TURNS, 0, LAST, False)
            score_step(FULL_TURNS - 1, 1, (CHUNKS - 2) * CHUNK, CHUNK)
            score_step(FULL_TURNS, 0, (CHUNKS - 1) * CHUNK, LAST)
            nc.scalar.mul(dst_score[:, NODES:PAD], ones[:, 0:PAD - NODES], 0.0).then_inc(score_done[0], 1)

            act.wait_ge(edge_kept, N_GROUPS)
            act.wait_ge(starts_loaded, 16)
            for j in range(SLOTS):
                nc.scalar.copy(idx_ring[:, j:j + 1], src_cols[:, j:j + 1]).then_inc(idx_first, 1)
            act.wait_ge(score_done[0], FULL_TURNS + 2)
            act.wait_ge(score_done[1], FULL_TURNS)

            def gate(turn, j, start, first):
                act.wait_ge(gathered[j], 16 * (turn + 1))
                nc.scalar.copy(idx_ring[:, j:j + 1], src_cols[:, bass.ds((turn + 1) * SLOTS + j, 1)]
                               ).then_inc(idx_ready[j], 1)
                if not first:
                    act.wait_ge(mask_ready[j], turn)
                nc.scalar.activation(gate_ring[:, j, :], dst_score[:, bass.ds(start, P)], ACT.Sigmoid,
                                     bias=row_ring[:, j, D:ROW]).then_inc(gate_ready[j], 1)

            def window_starts(turn):
                regs = [act.value_load(starts[0:1, bass.ds(turn * SLOTS + j, 1)], min_val=0, max_val=NODES)
                        for j in range(SLOTS)]
                return regs

            first_starts = window_starts(0)
            for j in range(SLOTS):
                gate(0, j, first_starts[j], True)
            with act.Fori(1, TURNS) as turn:
                now = window_starts(turn)
                for j in range(SLOTS):
                    gate(turn, j, now[j], False)

            def rz_step(turn, b, width, first):
                act.wait_ge(gru_done[b], turn + 1)
                if not first:
                    act.wait_ge(t_done[b], turn)
                nc.scalar.activation(r_sb[:, b, 0:width], ps[:, 4 * b, 0:width], ACT.Sigmoid,
                                     bias=b_rz[:, 0:1]).then_inc(r_done[b], 1)
                if not first:
                    act.wait_ge(e_done[b], turn)
                nc.scalar.activation(z_sb[:, b, 0:width], ps[:, 4 * b + 1, 0:width], ACT.Sigmoid,
                                     bias=b_rz[:, 1:2]).then_inc(zg_done[b], 1)

            def n_step(turn, b, width, first):
                act.wait_ge(u_done[b], turn + 1)
                if not first:
                    act.wait_ge(new_done[b], turn)
                nc.scalar.activation(n_sb[:, b, 0:width], t_sb[:, b, 0:width], ACT.Tanh,
                                     bias=b_gates[:, 2:3]).then_inc(n_done[b], 1)

            for b in range(2):
                rz_step(0, b, CHUNK, True)
                n_step(0, b, CHUNK, True)
            with act.Fori(1, FULL_TURNS) as turn:
                for b in range(2):
                    rz_step(turn, b, CHUNK, False)
                    n_step(turn, b, CHUNK, False)
            rz_step(FULL_TURNS, 0, LAST, False)
            n_step(FULL_TURNS, 0, LAST, False)

            act.wait_ge(bn_line, 1)
            nc.scalar.activation(bn[:, 0:1], bn_mv[:, 1:2], ACT.Sqrt, bias=eps[:, 0:1]).then_inc(bn_std, 1)
            act.wait_ge(bn_line, 5)

            def y_step(turn, b, start, width, first):
                if not first:
                    act.wait_ge(y_turned[b], turn)
                nc.scalar.activation(n_sb[:, b, 0:width], agg[:, bass.ds(start, width)], ACT.Identity,
                                     bias=bn[:, 3:4], scale=bn[:, 2:3]).then_inc(y_done[b], 1)

            y_step(0, 0, 0, CHUNK, True)
            y_step(0, 1, CHUNK, CHUNK, True)
            with act.Fori(1, FULL_TURNS) as turn:
                for b in range(2):
                    y_step(turn, b, (2 * turn + b) * CHUNK, CHUNK, False)
            y_step(FULL_TURNS, 0, (CHUNKS - 1) * CHUNK, LAST, False)

        @block.vector
        def _(dve):
            line = [0]

            def link(ins):
                line[0] += 1
                ins.then_inc(dve_line, 1)
                dve.wait_ge(dve_line, line[0])

            dst3 = dst_f.rearrange("p (c e) -> p c e", e=P)
            rel3 = dst_rel.rearrange("p (c e) -> p c e", e=P)
            dve.wait_ge(edges_loaded, 32)
            nc.vector.tensor_copy(src_f, src_int)
            link(nc.vector.tensor_copy(dst_f, dst_int))
            nc.vector.tensor_copy(first_f[:, :], dst3[:, :, 0])
            nc.vector.tensor_copy(first_i[:, :], dst3[:, :, 0]).then_inc(starts_made, 1)
            link(nc.vector.tensor_tensor(span_f[:, :], dst3[:, :, P - 1], dst3[:, :, 0], ALU.subtract))
            link(nc.vector.tensor_copy(span_i[:, :], span_f[:, :]))
            nc.vector.tensor_tensor(rel3, dst3, first_f[:, :].unsqueeze(2).broadcast_to((ROWS, COLS, P)), ALU.subtract
                                    ).then_inc(rel_made, 1)
            link(nc.vector.tensor_scalar(more_i[:, :], span_i[:, :], P.bit_length() - 1, None, ALU.arith_shift_right))
            link(nc.vector.tensor_copy(more_f[:, :], more_i[:, :]))
            dve.wait_ge(consts_made, 8)
            nc.vector.tensor_tensor_scan(more_sum[:, :], ones[0:ROWS, 0:COLS], more_f[:, :], 0.0, ALU.mult, ALU.add
                                         ).then_inc(prefix_done, 1)
            dve.wait_ge(prefix_done, 2)
            link(nc.vector.tensor_copy(row_before[:, :], ps[0:ROWS, 7, 0:1]))
            link(nc.vector.tensor_scalar(more_sum[:, :], more_sum[:, :], row_before[:, 0:1], None, ALU.add))
            link(nc.vector.tensor_tensor(
                within, more_sum[:, :].unsqueeze(1).broadcast_to((ROWS, EXTRA, COLS)),
                lane[0:ROWS, 0:EXTRA].unsqueeze(2).broadcast_to((ROWS, EXTRA, COLS)), ALU.is_le))
            link(nc.vector.tensor_tensor(
                within_x, within, more_f[:, :].unsqueeze(1).broadcast_to((ROWS, EXTRA, COLS)), ALU.mult))
            nc.vector.tensor_reduce(count[:, 0, :], within, AX_X, ALU.add)
            nc.vector.tensor_reduce(count[:, 1, :], within_x, AX_X, ALU.add).then_inc(counts_made, 1)
            dve.wait_ge(counts_summed, 1)
            tile_k, done_k = ps[0:EXTRA, 7, 8:9], ps[0:EXTRA, 7, 16:17]
            e = ex[0:EXTRA, :]
            nc.vector.tensor_scalar(ex_idx[0:EXTRA, :], tile_k, float(TILES - 1), None, ALU.min).then_inc(ex_idx_made, 1)
            nc.vector.tensor_scalar(e[:, 0:1], tile_k, float(TILES), None, ALU.is_ge)
            link(nc.vector.tensor_tensor(e[:, 1:2], lane_p[0:EXTRA, :], done_k, ALU.subtract))
            link(nc.vector.tensor_scalar(e[:, 1:2], e[:, 1:2], 1.0, float(P), ALU.add, ALU.mult))
            dve.wait_ge(ex_gathered, 32)
            link(nc.vector.tensor_copy(ex_f[0:EXTRA, :, :], ex_int[0:EXTRA, :, :]))
            link(nc.vector.tensor_tensor(e[:, 2:3], e[:, 1:2], ex_f[0:EXTRA, 1, 0:1], ALU.add))
            link(nc.vector.tensor_scalar(e[:, 3:4], e[:, 2:3], -1.0, float(NODES), ALU.mult, ALU.add))
            link(nc.vector.tensor_tensor(e[:, 4:5], e[:, 3:4], e[:, 0:1], ALU.mult))
            link(nc.vector.tensor_tensor(e[:, 5:6], e[:, 4:5], e[:, 2:3], ALU.add))
            nc.vector.tensor_copy(ex_start[0:EXTRA, :], e[:, 5:6]).then_inc(starts_made, 1)
            nc.vector.tensor_scalar(ex_rel[0:EXTRA, :], ex_f[0:EXTRA, 1, :], e[:, 5:6], None, ALU.subtract
                                    ).then_inc(ex_made, 1)
            kept = 0
            for cols_sb in (src_cols, dst_cols):
                for group in edge_groups:
                    kept += 1
                    dve.wait_ge(edge_turned, kept)
                    to = cols_sb[:, 0:TILES].rearrange("e (p c) -> e c p", c=COLS)[:, group[0]:group[-1] + 1, :]
                    nc.vector.tensor_copy(to, ps[:, 4 + kept % 2, 0:len(group) * P].rearrange("e (c p) -> e c p", p=P)[
                        :, :, 0:ROWS]).then_inc(edge_kept, 1)
            dve.wait_ge(edge_turned, N_GROUPS)
            nc.vector.tensor_copy(src_cols[:, TILES:STEPS], ps[:, 6, 0:EXTRA])
            nc.vector.tensor_copy(dst_cols[:, TILES:STEPS], ps[:, 6, P:P + EXTRA]).then_inc(edge_kept, 1)
            dve.wait_ge(consts_loaded, 16 * 15)
            nc.vector.tensor_scalar(w_att_dst_wide[:, :], ones[:, :], w_att_dst[:, 0:1], None, ALU.mult
                                    ).then_inc(wide_made, 1)
            nc.vector.tensor_tensor(b_rz[:, :], b_gates[:, 0:2], b_gates[:, 3:5], ALU.add)
            for g in range(2):
                dve.wait_ge(gates_turned, g + 1)
                nc.vector.tensor_copy(gates[:, 3 * g:3 * g + 3, :],
                                      ps[:, 6 + g, 0:3 * P].rearrange("p (g d) -> p g d", d=P)).then_inc(gates_kept, 1)

            def norm_step(turn, b, width, first):
                tiles = tiles_of(width)
                dve.wait_ge(x_loaded[b], 16 * (turn + (1 if width == CHUNK else len(tiles))))
                for j, n in tiles:
                    last = nc.vector.bn_stats(stats[0:n, b, j, :], xbuf[0:n, b, j, :])
                last.then_inc(stats_done[b], 1)
                dve.wait_ge(edges_loaded, 32)
                dve.wait_ge(stats_done[b], turn + 1)
                for j, n in tiles:
                    last = nc.vector.bn_aggr(mv[0:n, b, j, :], stats[0:n, b, j, :])
                last.then_inc(mv_done[b], 1)

            def z_step(turn, b, width, first):
                tiles = tiles_of(width)
                dve.wait_ge(std_done[b], turn + 1)
                nc.vector.reciprocal(rstd[:, b, 0:len(tiles)], std[:, b, 0:len(tiles)]).then_inc(rstd_done[b], 1)
                dve.wait_ge(rstd_done[b], turn + 1)
                if not first:
                    dve.wait_ge(z_turned[b], turn)
                for j, n in tiles:
                    last = nc.vector.tensor_scalar(zbuf[0:n, b, j, :], xbuf[0:n, b, j, :], mv[0:n, b, j, 0:1],
                                                   rstd[0:n, b, j:j + 1], ALU.subtract, ALU.mult)
                last.then_inc(z_done[b], 1)

            def rows_step(turn, b, width, first):
                dve.wait_ge(dense_done[b], turn + 1)
                if not first:
                    dve.wait_ge(table_stored[b], 16 * turn)
                for half in range(2):
                    tiles = tiles_of(width)[2 * half:2 * half + 2]
                    if not tiles:
                        continue
                    if width == CHUNK:
                        last = nc.vector.tensor_tensor(
                            rows_out[:, b, 2 * half:2 * half + 2, :],
                            ps[:, 4 + 2 * b + half, :].rearrange("p (t d) -> p t d", t=2)[:, :, 0:ROW],
                            b_table[:, :].unsqueeze(1).broadcast_to((P, 2, ROW)), ALU.add)
                        continue
                    for j, n in tiles:
                        last = nc.vector.tensor_tensor(
                            rows_out[0:n, b, j, :], ps[0:n, 4 + 2 * b + half, (j % 2) * 256:(j % 2) * 256 + ROW],
                            b_table[0:n, :], ALU.add)
                last.then_inc(rows_done[b], 1)

            norm_step(0, 0, CHUNK, True)
            z_step(0, 0, CHUNK, True)
            norm_step(0, 1, CHUNK, True)
            z_step(0, 1, CHUNK, True)
            rows_step(0, 0, CHUNK, True)
            norm_step(1, 0, CHUNK, False)
            z_step(1, 0, CHUNK, False)
            rows_step(0, 1, CHUNK, True)
            norm_step(1, 1, CHUNK, False)
            z_step(1, 1, CHUNK, False)
            rows_step(1, 0, CHUNK, False)
            with dve.Fori(2, FULL_TURNS) as turn:
                for b in range(2):
                    norm_step(turn, b, CHUNK, False)
                    z_step(turn, b, CHUNK, False)
                    rows_step(turn - 1 + b, 1 - b, CHUNK, False)
            norm_step(FULL_TURNS, 0, LAST, False)
            z_step(FULL_TURNS, 0, LAST, False)
            rows_step(FULL_TURNS - 1, 1, CHUNK, False)
            rows_step(FULL_TURNS, 0, LAST, False)

            def mask(turn, j, first):
                dve.wait_ge(gate_ready[j], turn + 1)
                if not first:
                    dve.wait_ge(summed[j], turn)
                nc.vector.scalar_tensor_tensor(
                    out=mask_ring[:, j, :], in0=lane[:, :], scalar=dst_cols[:, bass.ds(turn * SLOTS + j, 1)],
                    in1=gate_ring[:, j, :], op0=ALU.is_equal, op1=ALU.mult).then_inc(mask_ready[j], 1)

            def add(turn, j, start, first):
                dve.wait_ge(summed[j], turn + 1)
                if j:
                    dve.wait_ge(added[j - 1], turn + 1)
                elif not first:
                    dve.wait_ge(added[SLOTS - 1], turn)
                window = agg[:, bass.ds(start, P)]
                nc.vector.tensor_tensor(window, ps[:, j, 0:P], window, ALU.add).then_inc(added[j], 1)

            def window_starts(first_step, n):
                return [dve.value_load(starts[0:1, bass.ds(first_step + j, 1)], min_val=0, max_val=NODES)
                        for j in range(n)]

            dve.wait_ge(starts_loaded, 16)
            dve.wait_ge(agg_zeroed, 1)
            first_starts = window_starts(0, SLOTS)
            for j in range(SLOTS):
                mask(0, j, True)
                if j:
                    add(0, j - 1, first_starts[j - 1], True)
            with dve.Fori(1, TURNS) as turn:
                now = window_starts(turn * SLOTS - 1, SLOTS)
                for j in range(SLOTS):
                    mask(turn, j, False)
                    if j:
                        add(turn, j - 1, now[j], False)
                    else:
                        add(turn - 1, SLOTS - 1, now[0], False)
            add(TURNS - 1, SLOTS - 1, window_starts(STEPS - 1, 1)[0], False)

            def tu_step(turn, b, width, first):
                dve.wait_ge(r_done[b], turn + 1)
                if not first:
                    dve.wait_ge(n_done[b], turn)
                nc.vector.scalar_tensor_tensor(
                    out=t_sb[:, b, 0:width], in0=ps[:, 4 * b + 3, 0:width], scalar=b_gates[:, 5:6],
                    in1=r_sb[:, b, 0:width], op0=ALU.add, op1=ALU.mult).then_inc(t_done[b], 1)
                dve.wait_ge(t_done[b], turn + 1)
                nc.vector.tensor_tensor(t_sb[:, b, 0:width], ps[:, 4 * b + 2, 0:width], t_sb[:, b, 0:width],
                                        ALU.add).then_inc(u_done[b], 1)

            def new_step(turn, b, start, width, chunk):
                dve.wait_ge(n_done[b], turn + 1)
                dve.wait_ge(h_loaded[b], 16 * (turn + 1))
                h, z = hbuf[:, b, 0:width], z_sb[:, b, 0:width]
                new = agg[:, bass.ds(start, width)]
                nc.vector.tensor_tensor(h, h, n_sb[:, b, 0:width], ALU.subtract).then_inc(d_done[b], 1)
                dve.wait_ge(d_done[b], turn + 1)
                dve.wait_ge(zg_done[b], turn + 1)
                nc.vector.tensor_tensor(h, z, h, ALU.mult).then_inc(e_done[b], 1)
                dve.wait_ge(e_done[b], turn + 1)
                nc.vector.tensor_tensor(new, n_sb[:, b, 0:width], h, ALU.add).then_inc(new_done[b], 1)
                dve.wait_ge(new_done[b], turn + 1)
                nc.vector.bn_stats(bn_all[:, chunk, :], new).then_inc(bn_done[b], 1)

            tu_step(0, 0, CHUNK, True)
            tu_step(0, 1, CHUNK, True)
            new_step(0, 0, 0, CHUNK, 0)
            with dve.Fori(1, FULL_TURNS) as turn:
                for b in range(2):
                    tu_step(turn, b, CHUNK, False)
                    c = 2 * turn + b - 1
                    new_step(turn - 1 + b, 1 - b, c * CHUNK, CHUNK, c)
            tu_step(FULL_TURNS, 0, LAST, False)
            new_step(FULL_TURNS - 1, 1, (CHUNKS - 2) * CHUNK, CHUNK, CHUNKS - 2)
            new_step(FULL_TURNS, 0, (CHUNKS - 1) * CHUNK, LAST, CHUNKS - 1)

            dve.wait_ge(bn_done[0], FULL_TURNS + 1)
            dve.wait_ge(bn_done[1], FULL_TURNS)
            nc.vector.bn_aggr(bn_mv[:, :], bn_all[:, :, :].rearrange("p c s -> p (c s)")).then_inc(bn_line, 1)
            dve.wait_ge(bn_std, 1)
            nc.vector.reciprocal(bn[:, 1:2], bn[:, 0:1]).then_inc(bn_line, 1)
            dve.wait_ge(bn_line, 2)
            nc.vector.tensor_tensor(bn[:, 2:3], bn[:, 1:2], gamma_c[:, :], ALU.mult).then_inc(bn_line, 1)
            dve.wait_ge(bn_line, 3)
            nc.vector.tensor_tensor(bn[:, 3:4], bn_mv[:, 0:1], bn[:, 2:3], ALU.mult).then_inc(bn_line, 1)
            dve.wait_ge(bn_line, 4)
            nc.vector.tensor_tensor(bn[:, 3:4], beta_c[:, :], bn[:, 3:4], ALU.subtract).then_inc(bn_line, 1)

            dve.wait_ge(x_back, 32)

            def out_step(turn, b, first_tile, width, first):
                dve.wait_ge(y_turned[b], turn + 1)
                if not first:
                    dve.wait_ge(o_stored[b], 16 * turn)
                if width == CHUNK:
                    last = nc.vector.tensor_tensor(
                        xbuf[:, b, :, :], ps[:, b, :].rearrange("p (t d) -> p t d", d=D),
                        x_again[:, bass.ds(first_tile, TILES_PER_CHUNK), :], ALU.add)
                else:
                    for j, n in tiles_of(width):
                        last = nc.vector.tensor_tensor(xbuf[0:n, b, j, :], ps[0:n, b, j * P:(j + 1) * P],
                                                       x_again[0:n, first_tile + j, :], ALU.add)
                last.then_inc(o_done[b], 1)

            out_step(0, 0, 0, CHUNK, True)
            out_step(0, 1, TILES_PER_CHUNK, CHUNK, True)
            with dve.Fori(1, FULL_TURNS) as turn:
                for b in range(2):
                    out_step(turn, b, (2 * turn + b) * TILES_PER_CHUNK, CHUNK, False)
            out_step(FULL_TURNS, 0, (CHUNKS - 1) * TILES_PER_CHUNK, LAST, False)

        @block.tensor
        def _(pe):
            pe.wait_ge(prefix_done, 1)
            nc.tensor.matmul(ps[0:ROWS, 7, 0:1], before[0:ROWS, 0:ROWS], more_sum[:, COLS - 1:COLS],
                             start=True, stop=True).then_inc(prefix_done, 1)
            pe.wait_ge(counts_made, 1)
            nc.tensor.matmul(ps[0:EXTRA, 7, 8:9], count[:, 0, :], ones[0:ROWS, 0:1], start=True, stop=True)
            nc.tensor.matmul(ps[0:EXTRA, 7, 16:17], count[:, 1, :], ones[0:ROWS, 0:1], start=True, stop=True
                             ).then_inc(counts_summed, 1)
            turned = 0
            for edges in (src_f, dst_rel):
                for group in edge_groups:
                    turned += 1
                    if turned > 2:
                        pe.wait_ge(edge_kept, turned - 2)
                    for i, c in enumerate(group):
                        last = nc.tensor.transpose(ps[:, 4 + turned % 2, i * P:i * P + ROWS],
                                                   edges[:, c * P:(c + 1) * P], ident[0:ROWS, 0:ROWS])
                    last.then_inc(edge_turned, 1)
            pe.wait_ge(ex_made, 1)
            nc.tensor.transpose(ps[:, 6, 0:EXTRA], ex_f[0:EXTRA, 0, :], ident[0:EXTRA, 0:EXTRA])
            nc.tensor.transpose(ps[:, 6, P:P + EXTRA], ex_rel[0:EXTRA, :], ident[0:EXTRA, 0:EXTRA]
                                ).then_inc(edge_turned, 1)
            pe.wait_ge(consts_loaded, 16 * 15)
            pe.wait_ge(edge_kept, N_GROUPS)
            for g in range(2):
                for i in range(3):
                    last = nc.tensor.transpose(ps[:, 6 + g, i * P:(i + 1) * P], gates_nat[:, 3 * g + i, :], ident[:, :])
                last.then_inc(gates_turned, 1)
            pe.wait_ge(wide_made, 1)
            pe.wait_ge(gates_kept, 2)

            def turn_step(turn, b, width, first):
                pe.wait_ge(z_done[b], turn + 1)
                if not first:
                    pe.wait_ge(h_done[b], turn)
                for j, n in tiles_of(width):
                    last = nc.tensor.transpose(ps[:, b, j * P:j * P + n], zbuf[0:n, b, j, :], ident[0:n, 0:n])
                last.then_inc(z_turned[b], 1)

            def dense_step(turn, b, width, first):
                pe.wait_ge(h_done[b], turn + 1)
                if not first:
                    pe.wait_ge(rows_done[b], turn)
                    pe.wait_ge(score_done[b], turn)
                for j, n in tiles_of(width):
                    nc.tensor.matmul(ps[0:n, 4 + 2 * b + j // 2, (j % 2) * 256:(j % 2) * 256 + ROW],
                                     hbuf[:, b, j * P:j * P + n], w_table[:, :], start=True, stop=True)
                nc.tensor.matmul(ps[:, 2 + b, 0:width], w_att_dst_wide[:, :], hbuf[:, b, 0:width],
                                 start=True, stop=True).then_inc(dense_done[b], 1)

            turn_step(0, 0, CHUNK, True)
            turn_step(0, 1, CHUNK, True)
            dense_step(0, 0, CHUNK, True)
            turn_step(1, 0, CHUNK, False)
            dense_step(0, 1, CHUNK, True)
            turn_step(1, 1, CHUNK, False)
            dense_step(1, 0, CHUNK, False)
            with pe.Fori(2, FULL_TURNS) as turn:
                for b in range(2):
                    turn_step(turn, b, CHUNK, False)
                    dense_step(turn - 1 + b, 1 - b, CHUNK, False)
            turn_step(FULL_TURNS, 0, LAST, False)
            dense_step(FULL_TURNS - 1, 1, CHUNK, False)
            dense_step(FULL_TURNS, 0, LAST, False)

            def scatter(turn, j, first):
                pe.wait_ge(mask_ready[j], turn + 1)
                if not first:
                    pe.wait_ge(added[j], turn)
                nc.tensor.matmul(ps[:, j, 0:P], row_ring[:, j, 0:D], mask_ring[:, j, :],
                                 start=True, stop=True).then_inc(summed[j], 1)

            pe.wait_ge(rows_done[0], FULL_TURNS + 1)
            pe.wait_ge(rows_done[1], FULL_TURNS)
            pe.wait_ge(score_done[0], FULL_TURNS + 1)
            pe.wait_ge(score_done[1], FULL_TURNS)
            for j in range(SLOTS):
                scatter(0, j, True)
            with pe.Fori(1, TURNS) as turn:
                for j in range(SLOTS):
                    scatter(turn, j, False)

            def gru_step(turn, b, start, width, first):
                pe.wait_ge(h_loaded[b], 16 * (turn + 1))
                if not first:
                    pe.wait_ge(u_done[b], turn)
                    pe.wait_ge(zg_done[b], turn)
                a, h = agg[:, bass.ds(start, width)], hbuf[:, b, 0:width]
                for g in range(2):
                    nc.tensor.matmul(ps[:, 4 * b + g, 0:width], gates[:, g, :], a, start=True, stop=False)
                    nc.tensor.matmul(ps[:, 4 * b + g, 0:width], gates[:, 3 + g, :], h, start=False, stop=True)
                nc.tensor.matmul(ps[:, 4 * b + 3, 0:width], gates[:, 5, :], h, start=True, stop=True)
                nc.tensor.matmul(ps[:, 4 * b + 2, 0:width], gates[:, 2, :], a, start=True, stop=True
                                 ).then_inc(gru_done[b], 1)

            pe.wait_ge(added[SLOTS - 1], TURNS)
            gru_step(0, 0, 0, CHUNK, True)
            gru_step(0, 1, CHUNK, CHUNK, True)
            with pe.Fori(1, FULL_TURNS) as turn:
                for b in range(2):
                    gru_step(turn, b, (2 * turn + b) * CHUNK, CHUNK, False)
            gru_step(FULL_TURNS, 0, (CHUNKS - 1) * CHUNK, LAST, False)

            def back_step(turn, b, width, first):
                pe.wait_ge(y_done[b], turn + 1)
                if not first:
                    pe.wait_ge(o_done[b], turn)
                for j, n in tiles_of(width):
                    last = nc.tensor.transpose(ps[0:n, b, j * P:(j + 1) * P], n_sb[:, b, j * P:j * P + n], ident[:, :])
                last.then_inc(y_turned[b], 1)

            back_step(0, 0, CHUNK, True)
            back_step(0, 1, CHUNK, True)
            with pe.Fori(1, FULL_TURNS) as turn:
                for b in range(2):
                    back_step(turn, b, CHUNK, False)
            back_step(FULL_TURNS, 0, LAST, False)


_INS = ['x', 'src', 'dst', 'L0_gnn_W_msg', 'L0_gnn_b_msg', 'L0_gnn_W_att', 'L0_gnn_b_att', 'L0_gnn_W_ih',
        'L0_gnn_b_ih', 'L0_gnn_W_hh', 'L0_gnn_b_hh', 'L0_gnn_gamma', 'L0_gnn_beta']


def kernel(**inputs):
    import numpy as _np
    import concourse.bacc as _bacc
    from concourse import mybir as _mybir
    from concourse.bass_utils import run_bass_kernel_spmd as _run

    nc = _bacc.Bacc("TRN2", target_bir_lowering=False, num_devices=1)
    arrays, args = {}, []
    for name in _INS:
        a = _np.ascontiguousarray(inputs[name])
        arrays[f"in_{name}_dram"] = a
        args.append(nc.dram_tensor(f"in_{name}_dram", a.shape, _mybir.dt.from_np(a.dtype), kind="ExternalInput").ap())
    shape = inputs['x'].shape
    args.append(nc.dram_tensor("out_0_dram", shape, _mybir.dt.float32, kind="ExternalOutput").ap())
    gnn_program(nc, *args)
    r = _run(nc, [arrays], core_ids=[0])
    return r.results[0]["out_0_dram"]
```

```python
from contextlib import ExitStack

import concourse.bass as bass
from concourse import mybir

F32 = mybir.dt.float32
I32 = mybir.dt.int32
U32 = mybir.dt.uint32
ALU = mybir.AluOpType
ACT = mybir.ActivationFunctionType
AX_X = mybir.AxisListType.X
ENGINE = mybir.EngineType

P = 128
SLOTS = 8
CHUNK = 512
TPC = CHUNK // P
PER_TURN = 4
EPS = 1e-5
BOUNDED = "node ids and counts of blocks: 0 to the number of nodes by their definition"


def up(n, m):
    return -(-n // m) * m


def tiles_of(width):
    return [(j, min(P, width - j * P)) for j in range(-(-width // P))]


def uses(turn, b, ring):
    return turn * (PER_TURN // ring) + b // ring


def back(turn, b, k):
    return (turn, b - k) if b >= k else (turn - 1, b - k + PER_TURN)


def wait_reuse(engine, semaphore, times):
    if not (isinstance(times, int) and times == 0):
        engine.wait_ge(semaphore, times)


def gnn_program(nc, x, src, dst, W_msg, b_msg, W_att, b_att, W_ih, b_ih, W_hh, b_hh, gamma, beta, out):
    NODES, D = x.shape
    EDGES = src.shape[0]
    assert D == P and EDGES % P == 0
    TILES = EDGES // P
    ROWS = next(r for r in range(P, 0, -1) if TILES % r == 0)
    COLS = TILES // ROWS
    STEPS = up(TILES, SLOTS)
    TURNS = STEPS // SLOTS
    EXTRA = up((NODES - 1) // P, SLOTS)
    EXTRA_TURNS = EXTRA // SLOTS
    assert EXTRA <= P and 0 < TILES % SLOTS
    ROW = D + 1
    REC = 12
    READY = SLOTS
    PAD = NODES + P
    CHUNKS = -(-NODES // CHUNK)
    LAST = NODES - (CHUNKS - 1) * CHUNK
    FULL_TURNS = (CHUNKS - 1) // PER_TURN
    assert (CHUNKS - 1) % PER_TURN == 0 and FULL_TURNS > 1
    assert COLS == CHUNKS
    BLOCKS = -(-NODES // P)
    LAST_BLOCK = NODES - (BLOCKS - 1) * P

    table = nc.dram_tensor("node_table", (NODES, ROW), F32, kind="Internal").ap()
    hT_dram = nc.dram_tensor("hT_spill", (P, NODES), F32, kind="Internal").ap()
    ex_starts_dram = nc.dram_tensor("extra_starts", (EXTRA, 1), I32, kind="Internal").ap()

    def width_of(c):
        return LAST if isinstance(c, int) and c == CHUNKS - 1 else CHUNK

    with ExitStack() as ctx:
        def sb(name, shape, dt=F32):
            return ctx.enter_context(nc.sbuf_tensor(name, shape, dt))

        def sem(name):
            return ctx.enter_context(nc.semaphore(name))

        def sems(name, n):
            return [sem(f"{name}{i}") for i in range(n)]

        ident = sb("ident", [P, P])
        ones = sb("ones", [P, P])
        before = sb("before", [P, P])
        lane = sb("lane", [P, P])
        lane_p = sb("lane_p", [P, 1])
        eps = sb("eps", [P, 1])
        w_table = sb("w_table", [P, ROW])
        w_att_dst = sb("w_att_dst", [P, 1])
        w_att_dst_wide = sb("w_att_dst_wide", [P, P])
        b_table = sb("b_table", [P, ROW])
        b_att_all = sb("b_att_all", [P, 1])
        gates_nat = sb("gates_nat", [P, 6, P])
        gates = sb("gates", [P, 6, P])
        b_gates = sb("b_gates", [P, 6])
        b_rz = sb("b_rz", [P, 2])
        gamma_c = sb("gamma_c", [P, 1])
        beta_c = sb("beta_c", [P, 1])

        src_cols = sb("src_cols", [P, STEPS + EXTRA + SLOTS])
        dst_cols = sb("dst_cols", [P, STEPS + EXTRA])
        records = sb("records", [1, TURNS + EXTRA_TURNS, REC], I32)
        agg = sb("agg", [P, PAD])
        region = sb("region", [P, max(PAD, CHUNKS * CHUNK)])
        dst_score = region[:, 0:PAD]
        x_again = region[:, 0:CHUNKS * CHUNK].rearrange("p (t d) -> p t d", d=D)

        first_i = sb("first_i", [ROWS, COLS], I32)
        last_i = sb("last_i", [ROWS, COLS], I32)
        more_i = sb("more_i", [ROWS, COLS], I32)
        more_f = sb("more_f", [ROWS, COLS])
        more_row = sb("more_row", [ROWS, 1])
        more_all = sb("more_all", [1, 1], I32)
        none_more = sb("none_more", [1, 1])
        more_sum = sb("more_sum", [ROWS, COLS])
        row_before = sb("row_before", [ROWS, 1])
        at_or_below = sb("at_or_below", [ROWS, EXTRA])
        count = sb("count", [ROWS, 2, EXTRA])
        ex = sb("ex", [P, 8])
        ex_idx = sb("ex_idx", [P, 1], U32)
        ex_start = sb("ex_start", [P, 1], I32)
        ex_int = sb("ex_int", [P, 2, P], I32)
        ex_f = sb("ex_f", [P, 2, P])

        xbuf = sb("xbuf", [P, 4, TPC, P])
        zbuf = sb("zbuf", [P, 2, TPC, P])
        hbuf = sb("hbuf", [P, 2, CHUNK])
        rows_out = sb("rows_out", [P, 2, TPC, ROW])
        stats = sb("stats", [P, 2, TPC, 6])
        mv = sb("mv", [P, 2, TPC, 2])
        std = sb("std", [P, 2, TPC])
        rstd = sb("rstd", [P, 2, TPC])
        edge_int = sb("edge_int", [ROWS, 4, 2, P], I32)
        edge_f = sb("edge_f", [ROWS, 2, 2, P])

        idx_ring = sb("idx_ring", [P, SLOTS], U32)
        row_ring = sb("row_ring", [P, SLOTS, ROW])
        gate_ring = sb("gate_ring", [P, SLOTS, P])
        mask_ring = sb("mask_ring", [P, SLOTS, P])

        h_blk = sb("h_blk", [P, P])
        r_blk = sb("r_blk", [P, P])
        z_blk = sb("z_blk", [P, P])
        t_blk = sb("t_blk", [P, P])
        n_blk = sb("n_blk", [P, P])
        bn_all = sb("bn_all", [P, BLOCKS, 6])
        bn_mv = sb("bn_mv", [P, 2])
        bn = sb("bn", [P, 4])

        ps = ctx.enter_context(nc.psum_tensor("ps", [P, 8, 512], F32))
        def ps_rows(b, j):
            return ps[:, 2 + 2 * b + j // 2, (j % 2) * 256:(j % 2) * 256 + ROW]

        BANKS = 4

        def ps_slot(j):
            return ps[:, j % BANKS, 0:P]

        R_SUM, Z_SUM, I_N, H_N = (slice(g * P, (g + 1) * P) for g in range(4))

        table_consts = sem("table_consts")
        gru_consts = sem("gru_consts")
        firsts_loaded = sem("firsts_loaded")
        records_loaded = sem("records_loaded")
        consts_made = sem("consts_made")
        waits_passed = sem("waits_passed")
        wide_made = sem("wide_made")
        dve_line = sem("dve_line")
        more_counted = sem("more_counted")
        more_totalled = sem("more_totalled")
        records_made = sem("records_made")
        gates_turned = sem("gates_turned")
        gates_kept = sem("gates_kept")
        agg_zeroed = sem("agg_zeroed")

        x_loaded = sems("x_loaded", 4)
        edges_loaded = sems("edges_loaded", 4)
        stats_done = sems("stats_done", 2)
        mv_done = sems("mv_done", 2)
        std_done = sems("std_done", 2)
        rstd_done = sems("rstd_done", 2)
        z_done = sems("z_done", 4)
        z_turned = sems("z_turned", 2)
        h_done = sems("h_done", 2)
        rows_summed = sems("rows_summed", 2)
        score_summed = sem("score_summed")
        rows_done = sems("rows_done", 2)
        score_done = sem("score_done")
        table_stored = sems("table_stored", 2)
        h_stored = sems("h_stored", 2)
        edges_made = sems("edges_made", 2)
        edges_turned = sem("edges_turned")
        edges_kept = sem("edges_kept")

        idx_first = sem("idx_first")
        idx_ready = sems("idx_ready", SLOTS)
        gathered = sems("gathered", SLOTS)
        gate_ready = sems("gate_ready", SLOTS)
        mask_ready = sems("mask_ready", SLOTS)
        summed = sems("summed", SLOTS)
        added = sems("added", SLOTS)

        prefix_made = sem("prefix_made")
        prefix_summed = sem("prefix_summed")
        ex_counted = sem("ex_counted")
        ex_counts_summed = sem("ex_counts_summed")
        ex_idx_made = sem("ex_idx_made")
        ex_gathered = sem("ex_gathered")
        ex_made = sem("ex_made")
        ex_turned = sem("ex_turned")
        ex_kept = sem("ex_kept")
        ex_stored = sem("ex_stored")
        ex_records = sem("ex_records")
        ex_idx_first = sem("ex_idx_first")

        h_loaded = sem("h_loaded")
        block_free = sem("block_free")
        gru_summed = sem("gru_summed")
        r_done = sem("r_done")
        z_gate_done = sem("z_gate_done")
        t_done = sem("t_done")
        u_done = sem("u_done")
        n_done = sem("n_done")
        d_done = sem("d_done")
        e_done = sem("e_done")
        new_done = sem("new_done")

        agg_complete = sem("agg_complete")
        x_back = sems("x_back", CHUNKS // 5)
        bn_line = sem("bn_line")
        bn_std = sem("bn_std")
        y_done = sems("y_done", 2)
        y_turned = sems("y_turned", 2)
        o_done = sems("o_done", 4)
        o_stored = sems("o_stored", 4)

        def record(turn, engine):
            _, values = nc.values_load_multi_w_load_instructions(
                records[0:1, bass.ds(turn, 1), 0:SLOTS + 1].rearrange("o t r -> o (t r)"), engines=[engine],
                min_val=0, max_val=NODES, skip_runtime_bounds_check_because=BOUNDED)
            return values

        def any_extra(eng, engine):
            _, (total,) = nc.values_load_multi_w_load_instructions(
                more_all[0:1, 0:1], engines=[engine], min_val=0, max_val=EXTRA,
                skip_runtime_bounds_check_because=BOUNDED)
            register = eng.alloc_register(f"extra_steps_{engine.name}")
            eng.reg_mov(register, total)
            return eng.If_ne(register, 0)

        block = ctx.enter_context(nc.Block())

        @block.sync
        def _(sp):
            def load_x(turn, b):
                c = PER_TURN * turn + b
                wait_reuse(sp, z_done[b], turn)
                if width_of(c) == CHUNK:
                    sp.dma_start(xbuf[:, b, :, :], x[bass.ds(c * CHUNK, CHUNK), :].rearrange("(t p) d -> p t d", p=P)
                                 ).then_inc(x_loaded[b], 16)
                else:
                    for j, n in tiles_of(LAST):
                        sp.dma_start(xbuf[0:n, b, j, :], x[c * CHUNK + j * P:c * CHUNK + j * P + n, :]
                                     ).then_inc(x_loaded[b], 16)

            def load_edges(turn, b):
                c = PER_TURN * turn + b
                done = uses(turn, b, 2) - 1
                wait_reuse(sp, edges_made[b % 2], max(done, 0) if isinstance(turn, int) else done)
                for i, edges in enumerate((src, dst)):
                    sp.dma_start(edge_int[:, b, i, :], edges.rearrange("(p c e) -> p c e", c=COLS, e=P)[
                        :, bass.ds(c, 1), :].rearrange("p o e -> p (o e)")).then_inc(edges_loaded[b], 16)

            def store_h(turn, b):
                c = PER_TURN * turn + b
                sp.wait_ge(h_done[b % 2], uses(turn, b, 2) + 1)
                sp.dma_start(hT_dram[:, bass.ds(c * CHUNK, width_of(c))], hbuf[:, b % 2, 0:width_of(c)]
                             ).then_inc(h_stored[b % 2], 16)

            def store_rows(turn, b):
                c = PER_TURN * turn + b
                sp.wait_ge(rows_done[b % 2], uses(turn, b, 2) + 1)
                if width_of(c) == CHUNK:
                    sp.dma_start(table[bass.ds(c * CHUNK, CHUNK), :].rearrange("(t p) d -> p t d", p=P),
                                 rows_out[:, b % 2, :, :]).then_inc(table_stored[b % 2], 16)
                else:
                    for j, n in tiles_of(LAST):
                        sp.dma_start(table[c * CHUNK + j * P:c * CHUNK + j * P + n, :],
                                     rows_out[0:n, b % 2, j, :]).then_inc(table_stored[b % 2], 16)

            def iteration(turn, b):
                c = PER_TURN * turn + b
                known = isinstance(turn, int)
                if not known or c + 3 < CHUNKS:
                    ahead = (turn, b + 3) if b + 3 < PER_TURN else (turn + 1, b + 3 - PER_TURN)
                    load_x(*ahead)
                if not known or 0 <= c - 1 < CHUNKS:
                    store_h(*back(turn, b, 1))
                if not known or c + 2 < CHUNKS:
                    load_edges(*((turn, b + 2) if b + 2 < PER_TURN else (turn + 1, b + 2 - PER_TURN)))
                if not known or 0 <= c - 2 < CHUNKS:
                    store_rows(*back(turn, b, 2))

            for b in range(3):
                load_x(0, b)
                if b < 2:
                    load_edges(0, b)
            sp.dma_start(w_table[:, 0:D], W_msg).then_inc(table_consts, 16)
            sp.dma_start(w_table[:, D:ROW], W_att[0:D, :]).then_inc(table_consts, 16)
            sp.dma_start(w_att_dst[:, :], W_att[D:2 * D, :]).then_inc(table_consts, 16)
            sp.dma_start(b_table[:, 0:D], b_msg.rearrange("(o d) -> o d", o=1).broadcast_to((P, D))
                         ).then_inc(table_consts, 16)
            sp.dma_start(b_att_all[:, :], b_att.rearrange("(o d) -> o d", o=1).broadcast_to((P, 1))
                         ).then_inc(table_consts, 16)
            for b in range(PER_TURN):
                iteration(0, b)
            by_row = dst.rearrange("(p c e) -> p c e", c=COLS, e=P)
            whole = TILES // SLOTS
            by_turn = dst[0:whole * SLOTS * P].rearrange("(o t e) -> o t e", o=1, e=SLOTS * P)
            rest = dst[whole * SLOTS * P:EDGES].rearrange("(o j e) -> o j e", o=1, e=P)
            sp.wait_ge(consts_made, 10)
            with nc.allow_non_contiguous_dma(reason="one destination per tile of edges"):
                sp.dma_start(first_i[:, :], by_row[:, :, 0]).then_inc(firsts_loaded, 16)
                sp.dma_start(last_i[:, :], by_row[:, :, P - 1]).then_inc(firsts_loaded, 16)
                for j in range(SLOTS):
                    sp.dma_start(records[0:1, 0:whole, j], by_turn[:, :, j * P]).then_inc(records_loaded, 16)
                sp.dma_start(records[0:1, whole, 0:TILES - whole * SLOTS], rest[:, :, 0]).then_inc(records_loaded, 16)
            with sp.Fori(1, FULL_TURNS - 1) as turn:
                for b in range(PER_TURN):
                    iteration(turn, b)
            sp.dma_start(gates_nat[:, 0:3, :], W_ih.rearrange("(g o) d -> o g d", o=P)).then_inc(gru_consts, 16)
            sp.dma_start(gates_nat[:, 3:6, :], W_hh.rearrange("(g o) d -> o g d", o=P)).then_inc(gru_consts, 16)
            for g in range(3):
                sp.dma_start(b_gates[:, g:g + 1], b_ih[g * P:(g + 1) * P].rearrange("(d o) -> d o", o=1)
                             ).then_inc(gru_consts, 16)
                sp.dma_start(b_gates[:, 3 + g:4 + g], b_hh[g * P:(g + 1) * P].rearrange("(d o) -> d o", o=1)
                             ).then_inc(gru_consts, 16)
            sp.dma_start(gamma_c[:, :], gamma.rearrange("(d o) -> d o", o=1)).then_inc(gru_consts, 16)
            sp.dma_start(beta_c[:, :], beta.rearrange("(d o) -> d o", o=1)).then_inc(gru_consts, 16)
            for c in range(CHUNKS - 1 - PER_TURN, CHUNKS + 2):
                iteration(c // PER_TURN, c % PER_TURN)

            sp.wait_ge(more_totalled, 2)
            with any_extra(sp, ENGINE.SP):
                sp.wait_ge(ex_made, 1)
                sp.dma_start(ex_starts_dram, ex_start[0:EXTRA, :]).then_inc(ex_stored, 16)
                sp.wait_ge(ex_stored, 16)
                sp.dma_start(records[0:1, TURNS:TURNS + EXTRA_TURNS, 0:SLOTS],
                             ex_starts_dram.rearrange("(o t j) k -> o t (j k)", o=1, j=SLOTS)).then_inc(ex_records, 16)

            sp.wait_ge(h_stored[0], 16 * (CHUNKS // 2 + 1))
            sp.wait_ge(h_stored[1], 16 * (CHUNKS // 2))
            with sp.Fori(0, BLOCKS - 1) as c:
                sp.wait_ge(block_free, c + 1)
                sp.dma_start(h_blk[:, :], hT_dram[:, bass.ds(c * P, P)]).then_inc(h_loaded, 16)
            sp.wait_ge(block_free, BLOCKS)
            sp.dma_start(h_blk[:, 0:LAST_BLOCK], hT_dram[:, NODES - LAST_BLOCK:NODES]).then_inc(h_loaded, 16)

            def store_out(turn, b):
                c = PER_TURN * turn + b
                sp.wait_ge(o_done[b], turn + 1)
                if width_of(c) == CHUNK:
                    sp.dma_start(out[bass.ds(c * CHUNK, CHUNK), :].rearrange("(t p) d -> p t d", p=P),
                                 xbuf[:, b, :, :]).then_inc(o_stored[b], 16)
                else:
                    for j, n in tiles_of(LAST):
                        sp.dma_start(out[c * CHUNK + j * P:c * CHUNK + j * P + n, :], xbuf[0:n, b, j, :]
                                     ).then_inc(o_stored[b], 16)

            with sp.Fori(0, FULL_TURNS) as turn:
                for b in range(PER_TURN):
                    store_out(turn, b)
            store_out(FULL_TURNS, 0)
            sp.wait_ge(o_stored[0], 16 * (FULL_TURNS + len(tiles_of(LAST))))
            for b in range(1, PER_TURN):
                sp.wait_ge(o_stored[b], 16 * FULL_TURNS)

        @block.gpsimd
        def _(pool):
            nc.gpsimd.memset(eps[:, :], EPS).then_inc(consts_made, 1)
            nc.gpsimd.memset(b_table[:, D:ROW], 0.0).then_inc(consts_made, 1)
            nc.gpsimd.memset(ones[:, :], 1.0).then_inc(consts_made, 1)
            nc.gpsimd.iota(lane[:, :], [[1, P]], base=0, channel_multiplier=0,
                           allow_small_or_imprecise_dtypes=True).then_inc(consts_made, 1)
            nc.gpsimd.iota(lane_p[:, :], [[0, 1]], base=0, channel_multiplier=1,
                           allow_small_or_imprecise_dtypes=True).then_inc(consts_made, 1)
            pool.wait_ge(consts_made, 5)
            nc.gpsimd.affine_select(out=ident[:, :], in_=ones[:, :], compare_op=ALU.is_equal, fill=0.0, base=0,
                                    pattern=[[1, P]], channel_multiplier=-1).then_inc(consts_made, 1)
            nc.gpsimd.affine_select(out=before[:, :], in_=ones[:, :], compare_op=ALU.is_gt, fill=0.0, base=0,
                                    pattern=[[1, P]], channel_multiplier=-1).then_inc(consts_made, 1)
            nc.gpsimd.memset(src_cols[:, TILES:], 0.0).then_inc(consts_made, 1)
            nc.gpsimd.memset(dst_cols[:, TILES:], -1.0).then_inc(consts_made, 1)
            nc.gpsimd.memset(records[:, TURNS - 1:, :], NODES).then_inc(consts_made, 1)

            def normalise(turn, b):
                c = PER_TURN * turn + b
                pool.wait_ge(rstd_done[b % 2], uses(turn, b, 2) + 1)
                wait_reuse(pool, z_turned[b % 2], uses(turn, b, 2))
                pool.sem_inc(waits_passed, 1)
                for j, n in tiles_of(width_of(c)):
                    last = nc.gpsimd.tensor_scalar(zbuf[0:n, b % 2, j, :], xbuf[0:n, b, j, :], mv[0:n, b % 2, j, 0:1],
                                                   rstd[0:n, b % 2, j:j + 1], ALU.subtract, ALU.mult)
                last.then_inc(z_done[b], 1)

            for b in range(PER_TURN):
                normalise(0, b)
            with pool.Fori(1, FULL_TURNS) as turn:
                for b in range(PER_TURN):
                    normalise(turn, b)
            normalise(FULL_TURNS, 0)

            last_stores = 16 * (CHUNKS // 2 + len(tiles_of(LAST)))

            def gather(j):
                nc.gpsimd.indirect_dma_start(
                    row_ring[:, j, :], None, table,
                    bass.IndirectOffsetOnAxis(ap=idx_ring[:, j:j + 1], axis=0)).then_inc(gathered[j], 16)

            def steps(turn):
                for j in range(SLOTS):
                    pool.wait_ge(table_stored[0], last_stores)
                    pool.wait_ge(idx_ready[j], turn)
                    pool.wait_ge(summed[j], turn)
                    gather(j)

            pool.wait_ge(table_stored[0], last_stores)
            pool.wait_ge(table_stored[1], 16 * (CHUNKS // 2))
            for j in range(SLOTS):
                pool.wait_ge(idx_first, j + 1)
                gather(j)
            with pool.Fori(1, TURNS) as turn:
                steps(turn)

            pool.wait_ge(more_totalled, 2)
            with any_extra(pool, ENGINE.Pool):
                pool.wait_ge(ex_idx_made, 1)
                for i, edges in enumerate((src, dst)):
                    nc.gpsimd.indirect_dma_start(
                        ex_int[0:EXTRA, i, :], None, edges.rearrange("(t e) -> t e", e=P),
                        bass.IndirectOffsetOnAxis(ap=ex_idx[0:EXTRA, :], axis=0)).then_inc(ex_gathered, 16)
                pool.wait_ge(ex_idx_first, SLOTS)
                with pool.Fori(TURNS, TURNS + EXTRA_TURNS) as turn:
                    steps(turn)

        @block.scalar
        def _(act):
            def iteration(turn, b):
                c = PER_TURN * turn + b
                known = isinstance(turn, int)
                r = b % 2
                if not known or c < CHUNKS:
                    n = len(tiles_of(width_of(c)))
                    act.wait_ge(mv_done[r], uses(turn, b, 2) + 1)
                    nc.scalar.activation(std[:, r, 0:n], mv[:, r, 0:n, 1], ACT.Sqrt, bias=eps[:, 0:1]
                                         ).then_inc(std_done[r], 1)
                if not known or 0 <= c - 2 < CHUNKS:
                    d, w = c - 2, width_of(c - 2)
                    act.wait_ge(score_summed, d + 1)
                    nc.scalar.activation(dst_score[:, bass.ds(d * CHUNK, w)], ps[:, 6, 0:w], ACT.Identity,
                                         bias=b_att_all[:, 0:1]).then_inc(score_done, 1)
                    act.wait_ge(edges_turned, d + 1)
                    for i, cols in enumerate((src_cols, dst_cols)):
                        last = nc.scalar.copy(cols[:, 0:TILES].rearrange("e (p c) -> e c p", c=COLS)[:, bass.ds(d, 1), :],
                                              ps[:, 7, i * P:i * P + ROWS].unsqueeze(1))
                    last.then_inc(edges_kept, 1)
                if not known or c < CHUNKS:
                    w = width_of(c)
                    act.wait_ge(z_turned[r], uses(turn, b, 2) + 1)
                    if not known or c >= 2:
                        act.wait_ge(h_stored[r], 16 * uses(turn, b, 2))
                        act.wait_ge(rows_summed[r], uses(turn, b, 2))
                    nc.scalar.activation(hbuf[:, r, 0:w], ps[:, r, 0:w], ACT.Relu).then_inc(h_done[r], 1)
                    piece = CHUNK if w == CHUNK else PAD - (CHUNKS - 1) * CHUNK
                    if piece == CHUNK:
                        nc.scalar.mul(agg[:, bass.ds(c * CHUNK, CHUNK)].rearrange("p (t d) -> p t d", d=P),
                                      ones[:, :].unsqueeze(1).broadcast_to((P, TPC, P)), 0.0).then_inc(agg_zeroed, 1)
                    else:
                        for a in range(c * CHUNK, PAD, P):
                            last = nc.scalar.mul(agg[:, a:min(a + P, PAD)], ones[:, 0:min(P, PAD - a)], 0.0)
                        last.then_inc(agg_zeroed, 1)

            act.wait_ge(consts_made, 10)
            act.wait_ge(table_consts, 16 * 5)
            for b in range(PER_TURN):
                iteration(0, b)
            with act.Fori(1, FULL_TURNS) as turn:
                for b in range(PER_TURN):
                    iteration(turn, b)
            for b in range(3):
                iteration(FULL_TURNS, b)
            nc.scalar.mul(dst_score[:, NODES:PAD], ones[:, 0:PAD - NODES], 0.0).then_inc(score_done, 1)

            act.wait_ge(edges_kept, COLS)
            for j in range(SLOTS):
                nc.scalar.copy(idx_ring[:, j:j + 1], src_cols[:, j:j + 1]).then_inc(idx_first, 1)
            act.wait_ge(records_made, 1)
            act.wait_ge(score_done, CHUNKS + 1)

            def gate(turn, j, start):
                act.wait_ge(gathered[j], 16 * (turn + 1))
                nc.scalar.copy(idx_ring[:, j:j + 1], src_cols[:, bass.ds((turn + 1) * SLOTS + j, 1)]
                               ).then_inc(idx_ready[j], 1)
                wait_reuse(act, mask_ready[j], turn)
                nc.scalar.activation(gate_ring[:, j, :], dst_score[:, bass.ds(start, P)], ACT.Sigmoid,
                                     bias=row_ring[:, j, D:ROW]).then_inc(gate_ready[j], 1)

            def gru_rz(c, w):
                act.wait_ge(gru_summed, c + 1)
                nc.scalar.activation(r_blk[:, 0:w], ps[:, 7, R_SUM][:, 0:w], ACT.Sigmoid, bias=b_rz[:, 0:1]
                                     ).then_inc(r_done, 1)
                nc.scalar.activation(z_blk[:, 0:w], ps[:, 7, Z_SUM][:, 0:w], ACT.Sigmoid, bias=b_rz[:, 1:2]
                                     ).then_inc(z_gate_done, 1)

            def gru_n(c, w):
                act.wait_ge(u_done, c + 1)
                nc.scalar.activation(n_blk[:, 0:w], t_blk[:, 0:w], ACT.Tanh, bias=b_gates[:, 2:3]).then_inc(n_done, 1)

            blocks_through = act.alloc_register("act_blocks_through")
            act.reg_mov(blocks_through, 0)
            act.wait_ge(gates_kept, 3)
            starts = record(0, ENGINE.Activation)
            for j in range(SLOTS):
                gate(0, j, starts[j])
            with act.Fori(1, TURNS) as turn:
                starts = record(turn, ENGINE.Activation)
                for j in range(SLOTS):
                    gate(turn, j, starts[j])
                    if j == 4:
                        with act.If_lt(blocks_through, starts[READY]):
                            gru_rz(act.snap(blocks_through, min_val=0, max_val=BLOCKS - 2), P)
                    if j == 6:
                        with act.If_lt(blocks_through, starts[READY]):
                            gru_n(act.snap(blocks_through, min_val=0, max_val=BLOCKS - 2), P)
                            act.reg_add(blocks_through, blocks_through, 1)

            with any_extra(act, ENGINE.Activation):
                act.wait_ge(ex_kept, 1)
                for j in range(SLOTS):
                    nc.scalar.copy(idx_ring[:, j:j + 1], src_cols[:, STEPS + j:STEPS + j + 1]).then_inc(ex_idx_first, 1)
                act.wait_ge(ex_records, 16)
                with act.Fori(TURNS, TURNS + EXTRA_TURNS) as turn:
                    starts = record(turn, ENGINE.Activation)
                    for j in range(SLOTS):
                        gate(turn, j, starts[j])

            act.wait_ge(agg_complete, 1)
            for k in range(len(x_back)):
                a = k * 5 * CHUNK
                if a + 5 * CHUNK <= NODES:
                    act.dma_start(x_again[:, k * 5 * TPC:(k + 1) * 5 * TPC, :],
                                  x[a:a + 5 * CHUNK, :].rearrange("(t p) d -> p t d", p=P)).then_inc(x_back[k], 32)
                else:
                    whole = NODES // P
                    act.dma_start(x_again[:, k * 5 * TPC:whole, :],
                                  x[a:whole * P, :].rearrange("(t p) d -> p t d", p=P)).then_inc(x_back[k], 16)
                    act.dma_start(x_again[0:NODES - whole * P, whole, :], x[whole * P:NODES, :]
                                  ).then_inc(x_back[k], 16)
            with act.Fori(act.snap(blocks_through, min_val=0, max_val=BLOCKS - 2), BLOCKS - 1) as c:
                gru_rz(c, P)
                gru_n(c, P)
            gru_rz(BLOCKS - 1, LAST_BLOCK)
            gru_n(BLOCKS - 1, LAST_BLOCK)

            act.wait_ge(bn_line, 1)
            nc.scalar.activation(bn[:, 0:1], bn_mv[:, 1:2], ACT.Sqrt, bias=eps[:, 0:1]).then_inc(bn_std, 1)
            act.wait_ge(bn_line, 5)

            def scale_step(turn, b):
                c, r = PER_TURN * turn + b, b % 2
                w = width_of(c)
                wait_reuse(act, y_turned[r], uses(turn, b, 2))
                nc.scalar.activation(hbuf[:, r, 0:w], agg[:, bass.ds(c * CHUNK, w)], ACT.Identity,
                                     bias=bn[:, 3:4], scale=bn[:, 2:3]).then_inc(y_done[r], 1)

            for b in range(PER_TURN):
                scale_step(0, b)
            with act.Fori(1, FULL_TURNS) as turn:
                for b in range(PER_TURN):
                    scale_step(turn, b)
            scale_step(FULL_TURNS, 0)

        @block.vector
        def _(dve):
            line = [0]

            def link(ins):
                line[0] += 1
                ins.then_inc(dve_line, 1)
                dve.wait_ge(dve_line, line[0])

            def iteration(turn, b):
                c = PER_TURN * turn + b
                known = isinstance(turn, int)
                r = b % 2
                if not known or c < CHUNKS:
                    tiles = tiles_of(width_of(c))
                    dve.wait_ge(x_loaded[b], 16 * (turn + (1 if width_of(c) == CHUNK else len(tiles))))
                    for j, n in tiles:
                        last = nc.vector.bn_stats(stats[0:n, r, j, :], xbuf[0:n, b, j, :])
                    last.then_inc(stats_done[r], 1)
                    if not known or c >= 2:
                        t2, b2 = back(turn, b, 2)
                        dve.wait_ge(z_done[b2], t2 + 1)
                    dve.wait_ge(stats_done[r], uses(turn, b, 2) + 1)
                    dve.sem_inc(waits_passed, 1)
                    for j, n in tiles:
                        last = nc.vector.bn_aggr(mv[0:n, r, j, :], stats[0:n, r, j, :])
                    last.then_inc(mv_done[r], 1)
                if not known or 0 <= c - 1 < CHUNKS:
                    t1, b1 = back(turn, b, 1)
                    r1 = b1 % 2
                    dve.wait_ge(edges_loaded[b1], 32 * (t1 + 1))
                    wait_reuse(dve, edges_turned, max(c - 2, 0) if known else c - 2)
                    nc.vector.tensor_copy(edge_f[:, r1, 0, :], edge_int[:, b1, 0, :])
                    nc.vector.tensor_scalar(edge_f[:, r1, 1, :], edge_int[:, b1, 1, :], edge_int[:, b1, 1, 0:1], None,
                                            ALU.subtract).then_inc(edges_made[r1], 1)
                if not known or 0 <= c - 2 < CHUNKS:
                    d = c - 2
                    dve.wait_ge(rows_summed[r], uses(turn, b, 2))
                    if not known or d >= 2:
                        dve.wait_ge(table_stored[r], 16 * (uses(turn, b, 2) - 1))
                    if width_of(d) == CHUNK:
                        for half in range(2):
                            last = nc.vector.tensor_tensor(
                                rows_out[:, r, 2 * half:2 * half + 2, :],
                                ps[:, 2 + 2 * r + half, :].rearrange("p (t d) -> p t d", t=2)[:, :, 0:ROW],
                                b_table[:, :].unsqueeze(1).broadcast_to((P, 2, ROW)), ALU.add)
                    else:
                        for j, n in tiles_of(LAST):
                            last = nc.vector.tensor_tensor(rows_out[0:n, r, j, :], ps_rows(r, j)[0:n, :],
                                                           b_table[0:n, :], ALU.add)
                    last.then_inc(rows_done[r], 1)
                if not known or c < CHUNKS:
                    n = len(tiles_of(width_of(c)))
                    dve.wait_ge(std_done[r], uses(turn, b, 2) + 1)
                    nc.vector.reciprocal(rstd[:, r, 0:n], std[:, r, 0:n]).then_inc(rstd_done[r], 1)

            iteration(0, 0)
            dve.wait_ge(table_consts, 16 * 5)
            nc.vector.tensor_scalar(w_att_dst_wide[:, :], ones[:, :], w_att_dst[:, 0:1], None, ALU.mult
                                    ).then_inc(wide_made, 1)
            for b in range(1, PER_TURN):
                iteration(0, b)
            with dve.Fori(1, FULL_TURNS) as turn:
                for b in range(PER_TURN):
                    iteration(turn, b)
            for b in range(3):
                iteration(FULL_TURNS, b)

            dve.wait_ge(firsts_loaded, 32)
            link(nc.vector.tensor_tensor(more_i[:, :], last_i[:, :], first_i[:, :], ALU.subtract))
            link(nc.vector.tensor_scalar(more_i[:, :], more_i[:, :], P.bit_length() - 1, None, ALU.arith_shift_right))
            link(nc.vector.tensor_copy(more_f[:, :], more_i[:, :]))
            nc.vector.tensor_reduce(more_row[:, :], more_f[:, :], AX_X, ALU.add).then_inc(more_counted, 1)
            dve.wait_ge(more_totalled, 1)
            nc.vector.tensor_copy(more_all[0:1, :], ps[0:1, 7, 0:1])
            link(nc.vector.tensor_scalar(none_more[0:1, :], ps[0:1, 7, 0:1], 0.5, None, ALU.is_lt))
            dve.wait_ge(records_loaded, 16 * (SLOTS + 1))
            ready = records[0:1, 0:TURNS, READY]
            link(nc.vector.tensor_scalar(ready, records[0:1, 0:TURNS, 0], P.bit_length() - 1, None,
                                         ALU.arith_shift_right))
            nc.vector.tensor_scalar(ready, ready, float(BLOCKS - 2), none_more[0:1, 0:1], ALU.min, ALU.mult
                                    ).then_inc(records_made, 1)
            nc.vector.tensor_copy(row_before[0:1, :], none_more[0:1, :]).then_inc(more_totalled, 1)
            dve.wait_ge(gru_consts, 16 * 10)
            nc.vector.tensor_tensor(b_rz[:, :], b_gates[:, 0:2], b_gates[:, 3:5], ALU.add).then_inc(gates_kept, 1)
            for g in range(2):
                dve.wait_ge(gates_turned, g + 1)
                nc.vector.tensor_copy(gates[:, 3 * g:3 * g + 3, :],
                                      ps[:, 5 + g, 0:3 * P].rearrange("p (g d) -> p g d", d=P)).then_inc(gates_kept, 1)
            nc.vector.memset(bn[:, 0:4], 0.0).then_inc(block_free, 1)

            def mask(turn, j):
                dve.wait_ge(gate_ready[j], turn + 1)
                wait_reuse(dve, summed[j], turn)
                nc.vector.scalar_tensor_tensor(
                    out=mask_ring[:, j, :], in0=lane[:, :], scalar=dst_cols[:, bass.ds(turn * SLOTS + j, 1)],
                    in1=gate_ring[:, j, :], op0=ALU.is_equal, op1=ALU.mult).then_inc(mask_ready[j], 1)

            def add(turn, j, start):
                dve.wait_ge(summed[j], turn + 1)
                if j:
                    dve.wait_ge(added[j - 1], turn + 1)
                else:
                    wait_reuse(dve, added[SLOTS - 1], turn)
                window = agg[:, bass.ds(start, P)]
                nc.vector.tensor_tensor(window, ps_slot(j), window, ALU.add).then_inc(added[j], 1)

            def gru_tu(c, w):
                dve.wait_ge(r_done, c + 1)
                dve.wait_ge(z_gate_done, c + 1)
                nc.vector.scalar_tensor_tensor(out=t_blk[:, 0:w], in0=ps[:, 7, H_N][:, 0:w], scalar=b_gates[:, 5:6],
                                               in1=r_blk[:, 0:w], op0=ALU.add, op1=ALU.mult).then_inc(t_done, 1)
                dve.wait_ge(t_done, c + 1)
                nc.vector.tensor_tensor(t_blk[:, 0:w], ps[:, 7, I_N][:, 0:w], t_blk[:, 0:w], ALU.add
                                        ).then_inc(u_done, 1)

            def gru_new(c, w):
                dve.wait_ge(n_done, c + 1)
                dve.wait_ge(h_loaded, 16 * (c + 1))
                new = agg[:, bass.ds(c * P, w)]
                nc.vector.tensor_tensor(t_blk[:, 0:w], h_blk[:, 0:w], n_blk[:, 0:w], ALU.subtract).then_inc(d_done, 1)
                dve.wait_ge(d_done, c + 1)
                nc.vector.tensor_tensor(t_blk[:, 0:w], z_blk[:, 0:w], t_blk[:, 0:w], ALU.mult).then_inc(e_done, 1)
                dve.wait_ge(e_done, c + 1)
                nc.vector.tensor_tensor(new, n_blk[:, 0:w], t_blk[:, 0:w], ALU.add).then_inc(new_done, 1)
                dve.wait_ge(new_done, c + 1)
                nc.vector.bn_stats(bn_all[:, bass.ds(c, 1), :].rearrange("p o s -> p (o s)"), new
                                   ).then_inc(block_free, 1)

            blocks_through = dve.alloc_register("dve_blocks_through")
            dve.reg_mov(blocks_through, 0)
            dve.wait_ge(agg_zeroed, CHUNKS)
            dve.wait_ge(edges_kept, COLS)
            dve.wait_ge(records_made, 1)
            starts = record(0, ENGINE.DVE)
            for j in range(SLOTS):
                mask(0, j)
                if j:
                    add(0, j - 1, starts[j - 1])
            add(0, SLOTS - 1, starts[SLOTS - 1])
            with dve.Fori(1, TURNS) as turn:
                starts = record(turn, ENGINE.DVE)
                for j in range(SLOTS):
                    mask(turn, j)
                    if j:
                        add(turn, j - 1, starts[j - 1])
                    if j == 5:
                        with dve.If_lt(blocks_through, starts[READY]):
                            gru_tu(dve.snap(blocks_through, min_val=0, max_val=BLOCKS - 2), P)
                add(turn, SLOTS - 1, starts[SLOTS - 1])
                with dve.If_lt(blocks_through, starts[READY]):
                    gru_new(dve.snap(blocks_through, min_val=0, max_val=BLOCKS - 2), P)
                    dve.reg_add(blocks_through, blocks_through, 1)

            with any_extra(dve, ENGINE.DVE):
                nc.vector.tensor_tensor_scan(more_sum[:, :], ones[0:ROWS, 0:COLS], more_f[:, :], 0.0, ALU.mult, ALU.add
                                             ).then_inc(prefix_made, 1)
                dve.wait_ge(prefix_summed, 1)
                link(nc.vector.tensor_copy(row_before[:, :], ps[0:ROWS, 7, 0:1]))
                link(nc.vector.tensor_scalar(more_sum[:, :], more_sum[:, :], row_before[:, 0:1], None, ALU.add))
                link(nc.vector.memset(count[:, :, :], 0.0))
                for c in range(COLS):
                    link(nc.vector.tensor_scalar(at_or_below[:, :], lane[0:ROWS, 0:EXTRA], more_sum[:, c:c + 1], None,
                                                 ALU.is_ge))
                    nc.vector.tensor_tensor(count[:, 0, :], count[:, 0, :], at_or_below[:, :], ALU.add)
                    link(nc.vector.scalar_tensor_tensor(
                        out=count[:, 1, :], in0=at_or_below[:, :], scalar=more_f[:, c:c + 1], in1=count[:, 1, :],
                        op0=ALU.mult, op1=ALU.add))
                nc.vector.tensor_copy(row_before[:, :], count[:, 0, 0:1]).then_inc(ex_counted, 1)
                dve.wait_ge(ex_counts_summed, 1)
                tile_k, done_k = ps[0:EXTRA, 7, 8:9], ps[0:EXTRA, 7, 16:17]
                e = ex[0:EXTRA, :]
                nc.vector.tensor_scalar(ex_idx[0:EXTRA, :], tile_k, float(TILES - 1), None, ALU.min
                                        ).then_inc(ex_idx_made, 1)
                nc.vector.tensor_scalar(e[:, 0:1], tile_k, float(TILES), None, ALU.is_ge)
                link(nc.vector.tensor_tensor(e[:, 1:2], lane_p[0:EXTRA, :], done_k, ALU.subtract))
                link(nc.vector.tensor_scalar(e[:, 1:2], e[:, 1:2], 1.0, float(P), ALU.add, ALU.mult))
                dve.wait_ge(ex_gathered, 32)
                link(nc.vector.tensor_copy(ex_f[0:EXTRA, :, :], ex_int[0:EXTRA, :, :]))
                link(nc.vector.tensor_tensor(e[:, 2:3], e[:, 1:2], ex_f[0:EXTRA, 1, 0:1], ALU.add))
                link(nc.vector.tensor_scalar(e[:, 3:4], e[:, 2:3], -1.0, float(NODES), ALU.mult, ALU.add))
                link(nc.vector.tensor_tensor(e[:, 4:5], e[:, 3:4], e[:, 0:1], ALU.mult))
                link(nc.vector.tensor_tensor(e[:, 5:6], e[:, 4:5], e[:, 2:3], ALU.add))
                link(nc.vector.tensor_copy(ex_start[0:EXTRA, :], e[:, 5:6]))
                nc.vector.tensor_scalar(ex_f[0:EXTRA, 1, :], ex_f[0:EXTRA, 1, :], e[:, 5:6], None, ALU.subtract
                                        ).then_inc(ex_made, 1)
                dve.wait_ge(ex_turned, 1)
                nc.vector.tensor_copy(src_cols[:, STEPS:STEPS + EXTRA], ps[:, 6, 0:EXTRA])
                nc.vector.tensor_copy(dst_cols[:, STEPS:STEPS + EXTRA], ps[:, 6, P:P + EXTRA]).then_inc(ex_kept, 1)
                dve.wait_ge(ex_records, 16)
                dve.wait_ge(ex_kept, 1)
                with dve.Fori(TURNS, TURNS + EXTRA_TURNS) as turn:
                    starts = record(turn, ENGINE.DVE)
                    for j in range(SLOTS):
                        mask(turn, j)
                        add(turn, j, starts[j])

            nc.vector.memset(bn[:, 0:4], 0.0).then_inc(agg_complete, 1)
            with dve.Fori(dve.snap(blocks_through, min_val=0, max_val=BLOCKS - 2), BLOCKS - 1) as c:
                gru_tu(c, P)
                gru_new(c, P)
            gru_tu(BLOCKS - 1, LAST_BLOCK)
            gru_new(BLOCKS - 1, LAST_BLOCK)

            dve.wait_ge(block_free, BLOCKS + 1)
            nc.vector.bn_aggr(bn_mv[:, :], bn_all[:, :, :].rearrange("p c s -> p (c s)")).then_inc(bn_line, 1)
            dve.wait_ge(bn_std, 1)
            nc.vector.reciprocal(bn[:, 1:2], bn[:, 0:1]).then_inc(bn_line, 1)
            dve.wait_ge(bn_line, 2)
            nc.vector.tensor_tensor(bn[:, 2:3], bn[:, 1:2], gamma_c[:, :], ALU.mult).then_inc(bn_line, 1)
            dve.wait_ge(bn_line, 3)
            nc.vector.tensor_tensor(bn[:, 3:4], bn_mv[:, 0:1], bn[:, 2:3], ALU.mult).then_inc(bn_line, 1)
            dve.wait_ge(bn_line, 4)
            nc.vector.tensor_tensor(bn[:, 3:4], beta_c[:, :], bn[:, 3:4], ALU.subtract).then_inc(bn_line, 1)

            def out_step(turn, b):
                c, r = PER_TURN * turn + b, b % 2
                dve.wait_ge(y_turned[r], uses(turn, b, 2) + 1)
                wait_reuse(dve, o_stored[b], 16 * turn)
                if width_of(c) == CHUNK:
                    last = nc.vector.tensor_tensor(xbuf[:, b, :, :], ps[:, r, :].rearrange("p (t d) -> p t d", d=D),
                                                   x_again[:, bass.ds(c * TPC, TPC), :], ALU.add)
                else:
                    for j, n in tiles_of(LAST):
                        last = nc.vector.tensor_tensor(xbuf[0:n, b, j, :], ps[0:n, r, j * P:(j + 1) * P],
                                                       x_again[0:n, c * TPC + j, :], ALU.add)
                last.then_inc(o_done[b], 1)

            for k in range(len(x_back)):
                dve.wait_ge(x_back[k], 32)
            for b in range(PER_TURN):
                out_step(0, b)
            with dve.Fori(1, FULL_TURNS) as turn:
                for b in range(PER_TURN):
                    out_step(turn, b)
            out_step(FULL_TURNS, 0)

        @block.tensor
        def _(pe):
            def iteration(turn, b):
                c = PER_TURN * turn + b
                known = isinstance(turn, int)
                r = b % 2
                if not known or c < CHUNKS:
                    pe.wait_ge(z_done[b], turn + 1)
                    wait_reuse(pe, h_done[r], uses(turn, b, 2))
                    for j, n in tiles_of(width_of(c)):
                        last = nc.tensor.transpose(ps[:, r, j * P:j * P + n], zbuf[0:n, r, j, :], ident[0:n, 0:n])
                    last.then_inc(z_turned[r], 1)
                if not known or 0 <= c - 1 < CHUNKS:
                    t1, b1 = back(turn, b, 1)
                    d, r1, w = c - 1, b1 % 2, width_of(c - 1)
                    pe.wait_ge(edges_made[r1], uses(t1, b1, 2) + 1)
                    wait_reuse(pe, edges_kept, d)
                    for i in range(2):
                        last = nc.tensor.transpose(ps[:, 7, i * P:i * P + ROWS], edge_f[:, r1, i, :],
                                                   ident[0:ROWS, 0:ROWS])
                    last.then_inc(edges_turned, 1)
                    pe.wait_ge(h_done[r1], uses(t1, b1, 2) + 1)
                    wait_reuse(pe, score_done, d)
                    nc.tensor.matmul(ps[:, 6, 0:w], w_att_dst_wide[:, :], hbuf[:, r1, 0:w],
                                     start=True, stop=True).then_inc(score_summed, 1)
                    wait_reuse(pe, rows_done[r1], uses(t1, b1, 2))
                    for j, n in tiles_of(w):
                        last = nc.tensor.matmul(ps_rows(r1, j)[0:n, :], hbuf[:, r1, j * P:j * P + n], w_table[:, :],
                                                start=True, stop=True)
                    last.then_inc(rows_summed[r1], 1)

            pe.wait_ge(consts_made, 10)
            iteration(0, 0)
            pe.wait_ge(wide_made, 1)
            for b in range(1, PER_TURN):
                iteration(0, b)
            with pe.Fori(1, FULL_TURNS) as turn:
                for b in range(PER_TURN):
                    iteration(turn, b)
            for b in range(2):
                iteration(FULL_TURNS, b)
            pe.wait_ge(edges_kept, COLS)
            pe.wait_ge(score_done, CHUNKS)
            pe.wait_ge(rows_done[0], CHUNKS // 2 + 1)
            pe.wait_ge(rows_done[1], CHUNKS // 2)
            pe.wait_ge(more_counted, 1)
            nc.tensor.matmul(ps[:, 7, 0:1], ones[0:ROWS, :], more_row[:, :], start=True, stop=True
                             ).then_inc(more_totalled, 1)
            pe.wait_ge(gru_consts, 16 * 10)
            for g in range(2):
                for i in range(3):
                    last = nc.tensor.transpose(ps[:, 5 + g, i * P:(i + 1) * P], gates_nat[:, 3 * g + i, :], ident[:, :])
                last.then_inc(gates_turned, 1)
            pe.wait_ge(gates_kept, 3)
            pe.wait_ge(more_totalled, 2)
            pe.wait_ge(records_made, 1)

            def scatter(turn, j):
                pe.wait_ge(mask_ready[j], turn + 1)
                if j >= BANKS:
                    pe.wait_ge(added[j - BANKS], turn + 1)
                else:
                    wait_reuse(pe, added[j - BANKS + SLOTS], turn)
                nc.tensor.matmul(ps_slot(j), row_ring[:, j, 0:D], mask_ring[:, j, :],
                                 start=True, stop=True).then_inc(summed[j], 1)

            def gru(c, w):
                pe.wait_ge(h_loaded, 16 * (c + 1))
                pe.wait_ge(block_free, c + 1)
                a, h = agg[:, bass.ds(c * P, w)], h_blk[:, 0:w]
                for g, part in enumerate((R_SUM, Z_SUM)):
                    nc.tensor.matmul(ps[:, 7, part][:, 0:w], gates[:, 3 + g, :], h, start=True, stop=False)
                    nc.tensor.matmul(ps[:, 7, part][:, 0:w], gates[:, g, :], a, start=False, stop=True)
                nc.tensor.matmul(ps[:, 7, H_N][:, 0:w], gates[:, 5, :], h, start=True, stop=True)
                nc.tensor.matmul(ps[:, 7, I_N][:, 0:w], gates[:, 2, :], a, start=True, stop=True
                                 ).then_inc(gru_summed, 1)

            blocks_through = pe.alloc_register("pe_blocks_through")
            pe.reg_mov(blocks_through, 0)
            for j in range(SLOTS):
                scatter(0, j)
            with pe.Fori(1, TURNS) as turn:
                _, (complete,) = nc.values_load_multi_w_load_instructions(
                    records[0:1, bass.ds(turn, 1), READY:READY + 1].rearrange("o t r -> o (t r)"),
                    engines=[ENGINE.PE], min_val=0, max_val=NODES, skip_runtime_bounds_check_because=BOUNDED)
                for j in range(SLOTS):
                    scatter(turn, j)
                    if j == 1:
                        with pe.If_lt(blocks_through, complete):
                            pe.wait_ge(added[SLOTS - 1], turn)
                            gru(pe.snap(blocks_through, min_val=0, max_val=BLOCKS - 2), P)
                            pe.reg_add(blocks_through, blocks_through, 1)

            with any_extra(pe, ENGINE.PE):
                pe.wait_ge(prefix_made, 1)
                nc.tensor.matmul(ps[0:ROWS, 7, 0:1], before[0:ROWS, 0:ROWS], more_sum[:, COLS - 1:COLS],
                                 start=True, stop=True).then_inc(prefix_summed, 1)
                pe.wait_ge(ex_counted, 1)
                nc.tensor.matmul(ps[0:EXTRA, 7, 8:9], count[:, 0, :], ones[0:ROWS, 0:1], start=True, stop=True)
                nc.tensor.matmul(ps[0:EXTRA, 7, 16:17], count[:, 1, :], ones[0:ROWS, 0:1], start=True, stop=True
                                 ).then_inc(ex_counts_summed, 1)
                pe.wait_ge(ex_made, 1)
                for i in range(2):
                    last = nc.tensor.transpose(ps[:, 6, i * P:i * P + EXTRA], ex_f[0:EXTRA, i, :],
                                               ident[0:EXTRA, 0:EXTRA])
                last.then_inc(ex_turned, 1)
                with pe.Fori(TURNS, TURNS + EXTRA_TURNS) as turn:
                    for j in range(SLOTS):
                        scatter(turn, j)

            pe.wait_ge(agg_complete, 1)
            with pe.Fori(pe.snap(blocks_through, min_val=0, max_val=BLOCKS - 2), BLOCKS - 1) as c:
                gru(c, P)
            gru(BLOCKS - 1, LAST_BLOCK)

            def back_step(turn, b):
                c, r = PER_TURN * turn + b, b % 2
                pe.wait_ge(y_done[r], uses(turn, b, 2) + 1)
                if not isinstance(turn, int) or c >= 2:
                    t2, b2 = back(turn, b, 2)
                    pe.wait_ge(o_done[b2], t2 + 1)
                for j, n in tiles_of(width_of(c)):
                    last = nc.tensor.transpose(ps[0:n, r, j * P:(j + 1) * P], hbuf[:, r, j * P:j * P + n], ident[:, :])
                last.then_inc(y_turned[r], 1)

            for b in range(PER_TURN):
                back_step(0, b)
            with pe.Fori(1, FULL_TURNS) as turn:
                for b in range(PER_TURN):
                    back_step(turn, b)
            back_step(FULL_TURNS, 0)


_INS = ['x', 'src', 'dst', 'L0_gnn_W_msg', 'L0_gnn_b_msg', 'L0_gnn_W_att', 'L0_gnn_b_att', 'L0_gnn_W_ih',
        'L0_gnn_b_ih', 'L0_gnn_W_hh', 'L0_gnn_b_hh', 'L0_gnn_gamma', 'L0_gnn_beta']


def kernel(**inputs):
    import numpy as _np
    import concourse.bacc as _bacc
    from concourse import mybir as _mybir
    from concourse.bass_utils import run_bass_kernel_spmd as _run

    nc = _bacc.Bacc("TRN2", target_bir_lowering=False, num_devices=1)
    arrays, args = {}, []
    for name in _INS:
        a = _np.ascontiguousarray(inputs[name])
        arrays[f"in_{name}_dram"] = a
        args.append(nc.dram_tensor(f"in_{name}_dram", a.shape, _mybir.dt.from_np(a.dtype), kind="ExternalInput").ap())
    shape = inputs['x'].shape
    args.append(nc.dram_tensor("out_0_dram", shape, _mybir.dt.float32, kind="ExternalOutput").ap())
    gnn_program(nc, *args)
    r = _run(nc, [arrays], core_ids=[0])
    return r.results[0]["out_0_dram"]
```

```python
from contextlib import ExitStack

import concourse.bass as bass
from concourse import mybir

F32 = mybir.dt.float32
I32 = mybir.dt.int32
U32 = mybir.dt.uint32
ALU = mybir.AluOpType
ACT = mybir.ActivationFunctionType
AX_X = mybir.AxisListType.X
ENGINE = mybir.EngineType

P = 128
SLOTS = 16
RING = 4
LAG = 2
CHUNK = 512
TPC = CHUNK // P
PER_TURN = 4
EPS = 1e-5
BOUNDED = "node ids and counts of blocks: 0 to the number of nodes by their definition"


def up(n, m):
    return -(-n // m) * m


def tiles_of(width):
    return [(j, min(P, width - j * P)) for j in range(-(-width // P))]


def earlier(turn, j, k):
    return (j - k, turn + 1) if j >= k else (j - k + SLOTS, turn)


def buffer_free(turn, j):
    if j + 1 >= RING:
        return turn * SLOTS + (j + 1 - RING)
    return 0 if isinstance(turn, int) and turn == 0 else turn * SLOTS - (RING - 1 - j)


def uses(turn, b, ring):
    return turn * (PER_TURN // ring) + b // ring


def back(turn, b, k):
    return (turn, b - k) if b >= k else (turn - 1, b - k + PER_TURN)


def wait_reuse(engine, semaphore, times):
    if not (isinstance(times, int) and times == 0):
        engine.wait_ge(semaphore, times)


def gnn_program(nc, x, src, dst, W_msg, b_msg, W_att, b_att, W_ih, b_ih, W_hh, b_hh, gamma, beta, out):
    NODES, D = x.shape
    EDGES = src.shape[0]
    assert D == P and EDGES % P == 0
    TILES = EDGES // P
    ROWS = next(r for r in range(P, 0, -1) if TILES % r == 0)
    COLS = TILES // ROWS
    STEPS = up(TILES, SLOTS)
    TURNS = STEPS // SLOTS
    PADDED = STEPS - TILES
    EXTRA = up((NODES - 1) // P, SLOTS)
    EXTRA_TURNS = EXTRA // SLOTS
    assert EXTRA <= P and 0 < TILES % SLOTS
    RAW = TURNS // 2
    WHOLE = TILES // SLOTS
    ROW = D + 1
    PAD = NODES + P
    CHUNKS = -(-NODES // CHUNK)
    LAST = NODES - (CHUNKS - 1) * CHUNK
    FULL_TURNS = (CHUNKS - 1) // PER_TURN
    assert PER_TURN * PER_TURN == SLOTS and TURNS % 2 == 0 and PER_TURN * (CHUNKS - 1) < RAW <= PER_TURN * CHUNKS
    assert (CHUNKS - 1) % PER_TURN == 0 and FULL_TURNS > 2
    assert COLS == CHUNKS
    X_TILES = -(-NODES // P)
    BLOCKS = NODES // P
    LAST_BLOCK = NODES - (BLOCKS - 1) * P

    table = nc.dram_tensor("node_table", (NODES, ROW), F32, kind="Internal").ap()
    hT_dram = nc.dram_tensor("hT_spill", (P, NODES), F32, kind="Internal").ap()
    early_x_dram = nc.dram_tensor("early_x", (RAW * P, D), F32, kind="Internal").ap()
    early_rows_dram = nc.dram_tensor("early_rows", (RAW * P, ROW), F32, kind="Internal").ap()
    ex_starts_dram = nc.dram_tensor("extra_starts", (EXTRA, 1), I32, kind="Internal").ap()

    def early_of(c):
        return RAW - c * PER_TURN if isinstance(c, int) and c == CHUNKS - 1 else PER_TURN

    def width_of(c):
        return LAST if isinstance(c, int) and c == CHUNKS - 1 else CHUNK

    with ExitStack() as ctx:
        def sb(name, shape, dt=F32):
            return ctx.enter_context(nc.sbuf_tensor(name, shape, dt))

        def sem(name):
            return ctx.enter_context(nc.semaphore(name))

        def sems(name, n):
            return [sem(f"{name}{i}") for i in range(n)]

        ident = sb("ident", [P, P])
        ones = sb("ones", [P, P])
        before = sb("before", [P, P])
        lane = sb("lane", [P, P])
        lane_p = sb("lane_p", [P, 1])
        eps = sb("eps", [P, 1])
        w_table = sb("w_table", [P, ROW])
        w_att_dst = sb("w_att_dst", [P, 1])
        w_att_dst_wide = sb("w_att_dst_wide", [P, P])
        b_table = sb("b_table", [P, ROW])
        b_att_all = sb("b_att_all", [P, 1])
        gates_nat = sb("gates_nat", [P, 6, P])
        gates = sb("gates", [P, 6, P])
        b_gates = sb("b_gates", [P, 6])
        b_rz = sb("b_rz", [P, 2])
        gamma_c = sb("gamma_c", [P, 1])
        beta_c = sb("beta_c", [P, 1])

        src_cols = sb("src_cols", [P, STEPS + EXTRA + SLOTS])
        dst_cols = sb("dst_cols", [P, STEPS + EXTRA])
        starts_all = sb("starts_all", [1, STEPS + EXTRA], I32)
        complete_all = sb("complete_all", [1, TURNS], I32)
        agg = sb("agg", [P, PAD])
        region = sb("region", [P, max(PAD, CHUNKS * CHUNK)])
        dst_score = region[:, 0:PAD]
        x_again = region[:, 0:CHUNKS * CHUNK].rearrange("p (t d) -> p t d", d=D)

        first_i = sb("first_i", [ROWS, COLS], I32)
        last_i = sb("last_i", [ROWS, COLS], I32)
        more_i = sb("more_i", [ROWS, COLS], I32)
        more_f = sb("more_f", [ROWS, COLS])
        more_row = sb("more_row", [ROWS, 1])
        more_all = sb("more_all", [1, 1], I32)
        none_more = sb("none_more", [1, 1])
        more_sum = sb("more_sum", [ROWS, COLS])
        row_before = sb("row_before", [ROWS, 1])
        at_or_below = sb("at_or_below", [ROWS, EXTRA])
        count = sb("count", [ROWS, 2, EXTRA])
        ex = sb("ex", [P, 8])
        ex_idx = sb("ex_idx", [P, 1], U32)
        ex_start = sb("ex_start", [P, 1], I32)
        ex_int = sb("ex_int", [P, 2, P], I32)
        ex_f = sb("ex_f", [P, 2, P])

        xbuf = sb("xbuf", [P, 4, TPC, P])
        zbuf = sb("zbuf", [P, 2, TPC, P])
        hbuf = sb("hbuf", [P, 2, CHUNK])
        rows_out = sb("rows_out", [P, 2, TPC, ROW])
        stats = sb("stats", [P, 2, TPC, 6])
        mv = sb("mv", [P, 2, TPC, 2])
        std = sb("std", [P, 2, TPC])
        rstd = sb("rstd", [P, 2, TPC])
        edge_int = sb("edge_int", [ROWS, 4, 2, P], I32)
        edge_f = sb("edge_f", [ROWS, 2, 2, P])

        idx_ring = sb("idx_ring", [P, SLOTS], U32)
        row_ring = sb("row_ring", [P, SLOTS, ROW])
        gate_ring = sb("gate_ring", [P, RING, P])
        mask_ring = sb("mask_ring", [P, RING, P])

        early_cols = sb("early_cols", [P, RAW])
        early_x = sb("early_x_tile", [P, P])
        early_stats = sb("early_stats", [P, 6])
        early_mv = sb("early_mv", [P, 2])
        early_std = sb("early_std", [P, 1])
        early_rstd = sb("early_rstd", [P, 1])
        early_z = sb("early_z", [P, P])
        early_h = sb("early_h", [P, P])
        early_out = sb("early_out", [P, ROW])

        h_blk = sb("h_blk", [P, LAST_BLOCK])
        r_blk = sb("r_blk", [P, LAST_BLOCK])
        z_blk = sb("z_blk", [P, LAST_BLOCK])
        t_blk = sb("t_blk", [P, LAST_BLOCK])
        n_blk = sb("n_blk", [P, LAST_BLOCK])
        bn_all = sb("bn_all", [P, BLOCKS, 6])
        bn_mv = sb("bn_mv", [P, 2])
        bn = sb("bn", [P, 4])

        ps = ctx.enter_context(nc.psum_tensor("ps", [P, 8, 512], F32))
        def ps_rows(b, j):
            return ps[:, 2 + 2 * b + j // 2, (j % 2) * 256:(j % 2) * 256 + ROW]

        def ps_slot(j):
            return ps[:, j % RING, 0:P]

        def gru_sums(w):
            if w == P:
                return [ps[:, 7, g * P:(g + 1) * P] for g in range(4)]
            return [ps[:, 6 + g // 2, g % 2 * 256:g % 2 * 256 + w] for g in range(4)]

        table_consts = sem("table_consts")
        gru_consts = sem("gru_consts")
        firsts_loaded = sem("firsts_loaded")
        starts_loaded = sem("starts_loaded")
        consts_made = sem("consts_made")
        waits_passed = sem("waits_passed")
        wide_made = sem("wide_made")
        dve_line = sem("dve_line")
        more_counted = sem("more_counted")
        more_totalled = sem("more_totalled")
        complete_made = sem("complete_made")
        gates_turned = sem("gates_turned")
        gates_kept = sem("gates_kept")
        agg_zeroed = sem("agg_zeroed")

        x_loaded = sems("x_loaded", 4)
        edges_loaded = sems("edges_loaded", 4)
        stats_done = sems("stats_done", 2)
        mv_done = sems("mv_done", 2)
        std_done = sems("std_done", 2)
        rstd_done = sems("rstd_done", 2)
        z_done = sems("z_done", 4)
        z_turned = sems("z_turned", 2)
        h_done = sems("h_done", 2)
        rows_summed = sems("rows_summed", 2)
        score_summed = sem("score_summed")
        rows_done = sems("rows_done", 2)
        score_done = sem("score_done")
        table_stored = sems("table_stored", 2)
        h_stored = sems("h_stored", 2)
        src_made = sems("src_made", 2)
        dst_made = sems("dst_made", 2)
        edges_turned = sem("edges_turned")
        edges_kept = sem("edges_kept")

        idx_first = sem("idx_first")
        idx_ready = sems("idx_ready", SLOTS // RING)
        gathered = sems("gathered", SLOTS)
        summed = sems("summed", SLOTS)
        gates_ready = sem("gates_ready")
        masks_ready = sem("masks_ready")
        steps_added = sem("steps_added")

        early_src_loaded = sem("early_src_loaded")
        early_src_made = sem("early_src_made")
        early_src_turned = sem("early_src_turned")
        early_cols_made = sem("early_cols_made")
        early_idx_ready = sem("early_idx_ready")
        early_gathered = sems("early_gathered", PER_TURN)
        early_stored = sems("early_stored", PER_TURN)
        early_loaded = sem("early_loaded")
        early_stats_done = sem("early_stats_done")
        early_mv_done = sem("early_mv_done")
        early_std_done = sem("early_std_done")
        early_rstd_done = sem("early_rstd_done")
        early_z_done = sem("early_z_done")
        early_turned = sem("early_turned")
        early_h_done = sem("early_h_done")
        early_summed = sem("early_summed")
        early_rows_done = sem("early_rows_done")
        early_rows_stored = sem("early_rows_stored")
        early_rows_loaded = sem("early_rows_loaded")

        prefix_made = sem("prefix_made")
        prefix_summed = sem("prefix_summed")
        ex_counted = sem("ex_counted")
        ex_counts_summed = sem("ex_counts_summed")
        ex_idx_made = sem("ex_idx_made")
        ex_gathered = sem("ex_gathered")
        ex_made = sem("ex_made")
        ex_turned = sem("ex_turned")
        ex_kept = sem("ex_kept")
        ex_stored = sem("ex_stored")
        ex_starts_loaded = sem("ex_starts_loaded")
        ex_idx_first = sem("ex_idx_first")

        h_loaded = sem("h_loaded")
        block_free = sem("block_free")
        gru_summed = sem("gru_summed")
        r_done = sem("r_done")
        z_gate_done = sem("z_gate_done")
        gru_line = sem("gru_line")
        u_done = sem("u_done")
        n_done = sem("n_done")

        agg_complete = sem("agg_complete")
        x_back = sem("x_back")
        bn_line = sem("bn_line")
        bn_std = sem("bn_std")
        y_done = sem("y_done")
        y_turned = sem("y_turned")
        o_done = sems("o_done", 4)
        o_stored = sems("o_stored", 4)

        HALF = SLOTS // 2

        def count_padded(engine, *counters):
            for counter in counters:
                engine.sem_inc(counter, PADDED)

        def y_buffer(b):
            return hbuf[:, b, :] if b < 2 else zbuf[:, b - 2, :, :].rearrange("p t d -> p (t d)")

        def window_starts(turn, j, engine):
            _, values = nc.values_load_multi_w_load_instructions(
                starts_all[0:1, bass.ds(turn * SLOTS + j, HALF)], engines=[engine],
                min_val=0, max_val=NODES, skip_runtime_bounds_check_because=BOUNDED)
            return list(values)

        def complete_blocks(turn, engine):
            _, (complete,) = nc.values_load_multi_w_load_instructions(
                complete_all[0:1, bass.ds(turn, 1)], engines=[engine], min_val=0, max_val=NODES,
                skip_runtime_bounds_check_because=BOUNDED)
            return complete

        def any_extra(eng, engine):
            _, (total,) = nc.values_load_multi_w_load_instructions(
                more_all[0:1, 0:1], engines=[engine], min_val=0, max_val=EXTRA,
                skip_runtime_bounds_check_because=BOUNDED)
            register = eng.alloc_register(f"extra_steps_{engine.name}")
            eng.reg_mov(register, total)
            return eng.If_ne(register, 0)

        block = ctx.enter_context(nc.Block())

        @block.sync
        def _(sp):
            def load_x(turn, b):
                c = PER_TURN * turn + b
                wait_reuse(sp, z_done[b], turn)
                if width_of(c) == CHUNK:
                    sp.dma_start(xbuf[:, b, :, :], x[bass.ds(c * CHUNK, CHUNK), :].rearrange("(t p) d -> p t d", p=P)
                                 ).then_inc(x_loaded[b], 16)
                else:
                    for j, n in tiles_of(LAST):
                        sp.dma_start(xbuf[0:n, b, j, :], x[c * CHUNK + j * P:c * CHUNK + j * P + n, :]
                                     ).then_inc(x_loaded[b], 16)

            def load_edges(turn, b):
                c = PER_TURN * turn + b
                done = uses(turn, b, 2) - 1
                for made in (src_made, dst_made):
                    wait_reuse(sp, made[b % 2], max(done, 0) if isinstance(turn, int) else done)
                for i, edges in enumerate((src, dst)):
                    sp.dma_start(edge_int[:, b, i, :], edges.rearrange("(p c e) -> p c e", c=COLS, e=P)[
                        :, bass.ds(c, 1), :].rearrange("p o e -> p (o e)")).then_inc(edges_loaded[b], 16)

            def store_h(turn, b):
                c = PER_TURN * turn + b
                sp.wait_ge(h_done[b % 2], uses(turn, b, 2) + 1)
                sp.dma_start(hT_dram[:, bass.ds(c * CHUNK, width_of(c))], hbuf[:, b % 2, 0:width_of(c)]
                             ).then_inc(h_stored[b % 2], 16)

            def store_early(turn, b):
                c = PER_TURN * turn + b
                n = early_of(c)
                sp.wait_ge(early_gathered[b], 16 * (PER_TURN * turn + n))
                sp.dma_start(early_x_dram[bass.ds(c * PER_TURN * P, n * P), :].rearrange("(t p) d -> p t d", p=P),
                             row_ring[:, b * PER_TURN:b * PER_TURN + n, 0:D]).then_inc(early_stored[b], 16)

            def store_rows(turn, b):
                c = PER_TURN * turn + b
                sp.wait_ge(rows_done[b % 2], uses(turn, b, 2) + 1)
                if width_of(c) == CHUNK:
                    sp.dma_start(table[bass.ds(c * CHUNK, CHUNK), :].rearrange("(t p) d -> p t d", p=P),
                                 rows_out[:, b % 2, :, :]).then_inc(table_stored[b % 2], 16)
                else:
                    for j, n in tiles_of(LAST):
                        sp.dma_start(table[c * CHUNK + j * P:c * CHUNK + j * P + n, :],
                                     rows_out[0:n, b % 2, j, :]).then_inc(table_stored[b % 2], 16)

            def iteration(turn, b):
                c = PER_TURN * turn + b
                known = isinstance(turn, int)
                if not known or c + 2 < CHUNKS:
                    load_edges(*((turn, b + 2) if b + 2 < PER_TURN else (turn + 1, b + 2 - PER_TURN)))
                if not known or c + 3 < CHUNKS:
                    load_x(*((turn, b + 3) if b + 3 < PER_TURN else (turn + 1, b + 3 - PER_TURN)))
                if not known or 0 <= c - 1 < CHUNKS:
                    store_early(*back(turn, b, 1))
                if not known or 0 <= c - 2 < CHUNKS:
                    store_h(*back(turn, b, 2))
                if not known or 0 <= c - 3 < CHUNKS:
                    store_rows(*back(turn, b, 3))

            load_x(0, 0)
            src_by_turn = src[0:WHOLE * SLOTS * P].rearrange("(t s e) -> t s e", s=SLOTS, e=P)
            sp.dma_start(ex_int[0:WHOLE - RAW, 0, :], src_by_turn[RAW:WHOLE, SLOTS - 1, :]
                         ).then_inc(early_src_loaded, 16)
            for b in range(3):
                if b:
                    load_x(0, b)
                if b < 2:
                    load_edges(0, b)
            sp.dma_start(w_table[:, 0:D], W_msg).then_inc(table_consts, 16)
            sp.dma_start(w_table[:, D:ROW], W_att[0:D, :]).then_inc(table_consts, 16)
            sp.dma_start(w_att_dst[:, :], W_att[D:2 * D, :]).then_inc(table_consts, 16)
            sp.dma_start(b_table[:, 0:D], b_msg.rearrange("(o d) -> o d", o=1).broadcast_to((P, D))
                         ).then_inc(table_consts, 16)
            sp.dma_start(b_att_all[:, :], b_att.rearrange("(o d) -> o d", o=1).broadcast_to((P, 1))
                         ).then_inc(table_consts, 16)
            for b in range(PER_TURN):
                iteration(0, b)
            by_row = dst.rearrange("(p c e) -> p c e", c=COLS, e=P)
            with nc.allow_non_contiguous_dma(reason="one destination per tile of edges"):
                sp.dma_start(first_i[:, :], by_row[:, :, 0]).then_inc(firsts_loaded, 16)
                sp.dma_start(last_i[:, :], by_row[:, :, P - 1]).then_inc(firsts_loaded, 16)
                sp.dma_start(starts_all[:, 0:TILES], dst.rearrange("(o t e) -> o t e", o=1, e=P)[:, :, 0]
                             ).then_inc(starts_loaded, 16)
            with sp.Fori(1, FULL_TURNS - 1) as turn:
                for b in range(PER_TURN):
                    iteration(turn, b)
            sp.dma_start(gates_nat[:, 0:3, :], W_ih.rearrange("(g o) d -> o g d", o=P)).then_inc(gru_consts, 16)
            sp.dma_start(gates_nat[:, 3:6, :], W_hh.rearrange("(g o) d -> o g d", o=P)).then_inc(gru_consts, 16)
            for g in range(3):
                sp.dma_start(b_gates[:, g:g + 1], b_ih[g * P:(g + 1) * P].rearrange("(d o) -> d o", o=1)
                             ).then_inc(gru_consts, 16)
                sp.dma_start(b_gates[:, 3 + g:4 + g], b_hh[g * P:(g + 1) * P].rearrange("(d o) -> d o", o=1)
                             ).then_inc(gru_consts, 16)
            sp.dma_start(gamma_c[:, :], gamma.rearrange("(d o) -> d o", o=1)).then_inc(gru_consts, 16)
            sp.dma_start(beta_c[:, :], beta.rearrange("(d o) -> d o", o=1)).then_inc(gru_consts, 16)
            for c in range(CHUNKS - 1 - PER_TURN, CHUNKS + 3):
                iteration(c // PER_TURN, c % PER_TURN)

            sp.wait_ge(more_totalled, 2)
            with any_extra(sp, ENGINE.SP):
                sp.wait_ge(ex_made, 1)
                sp.dma_start(ex_starts_dram, ex_start[0:EXTRA, :]).then_inc(ex_stored, 16)
                sp.wait_ge(ex_stored, 16)
                sp.dma_start(starts_all[:, STEPS:STEPS + EXTRA],
                             ex_starts_dram.rearrange("(o t) k -> o (t k)", o=1)).then_inc(ex_starts_loaded, 16)

            sp.wait_ge(h_stored[0], 16 * (CHUNKS // 2 + 1))
            sp.wait_ge(h_stored[1], 16 * (CHUNKS // 2))
            def load_x_again(c, n):
                sp.dma_start(x_again[0:n, bass.ds(c, 1), :].rearrange("p o d -> p (o d)"),
                             x[bass.ds(c * P, n), :]).then_inc(x_back, 16)

            sp.wait_ge(block_free, 1)
            sp.dma_start(h_blk[:, 0:P], hT_dram[:, 0:P]).then_inc(h_loaded, 16)
            with sp.Fori(1, BLOCKS - 1) as c:
                sp.wait_ge(block_free, c + 1)
                sp.dma_start(h_blk[:, 0:P], hT_dram[:, bass.ds(c * P, P)]).then_inc(h_loaded, 16)
                load_x_again(c - 1, P)
            sp.wait_ge(block_free, BLOCKS)
            sp.dma_start(h_blk[:, 0:LAST_BLOCK], hT_dram[:, NODES - LAST_BLOCK:NODES]).then_inc(h_loaded, 16)
            load_x_again(BLOCKS - 2, P)
            sp.wait_ge(agg_complete, 1)
            for c in range(BLOCKS - 1, X_TILES):
                load_x_again(c, min(P, NODES - c * P))

            def store_out(turn, b):
                c = PER_TURN * turn + b
                sp.wait_ge(o_done[b], turn + 1)
                if width_of(c) == CHUNK:
                    sp.dma_start(out[bass.ds(c * CHUNK, CHUNK), :].rearrange("(t p) d -> p t d", p=P),
                                 xbuf[:, b, :, :]).then_inc(o_stored[b], 16)
                else:
                    for j, n in tiles_of(LAST):
                        sp.dma_start(out[c * CHUNK + j * P:c * CHUNK + j * P + n, :], xbuf[0:n, b, j, :]
                                     ).then_inc(o_stored[b], 16)

            with sp.Fori(0, FULL_TURNS) as turn:
                for b in range(PER_TURN):
                    store_out(turn, b)
            store_out(FULL_TURNS, 0)
            sp.wait_ge(o_stored[0], 16 * (FULL_TURNS + len(tiles_of(LAST))))
            for b in range(1, PER_TURN):
                sp.wait_ge(o_stored[b], 16 * FULL_TURNS)

        @block.gpsimd
        def _(pool):
            nc.gpsimd.memset(eps[:, :], EPS).then_inc(consts_made, 1)
            nc.gpsimd.memset(b_table[:, D:ROW], 0.0).then_inc(consts_made, 1)
            nc.gpsimd.memset(ones[:, :], 1.0).then_inc(consts_made, 1)
            nc.gpsimd.iota(lane[:, :], [[1, P]], base=0, channel_multiplier=0,
                           allow_small_or_imprecise_dtypes=True).then_inc(consts_made, 1)
            nc.gpsimd.iota(lane_p[:, :], [[0, 1]], base=0, channel_multiplier=1,
                           allow_small_or_imprecise_dtypes=True).then_inc(consts_made, 1)
            pool.wait_ge(consts_made, 5)
            nc.gpsimd.affine_select(out=ident[:, :], in_=ones[:, :], compare_op=ALU.is_equal, fill=0.0, base=0,
                                    pattern=[[1, P]], channel_multiplier=-1).then_inc(consts_made, 1)
            nc.gpsimd.affine_select(out=before[:, :], in_=ones[:, :], compare_op=ALU.is_gt, fill=0.0, base=0,
                                    pattern=[[1, P]], channel_multiplier=-1).then_inc(consts_made, 1)
            nc.gpsimd.memset(src_cols[:, TILES:], 0.0).then_inc(consts_made, 1)
            nc.gpsimd.memset(dst_cols[:, TILES:], -1.0).then_inc(consts_made, 1)
            nc.gpsimd.memset(starts_all[:, TILES:], NODES).then_inc(consts_made, 1)

            nc.gpsimd.memset(ex_f[0:RAW, 0, :], 0.0).then_inc(consts_made, 1)

            def gather_early(turn, b):
                c = PER_TURN * turn + b
                pool.wait_ge(early_idx_ready, c + 1)
                wait_reuse(pool, early_stored[b], 16 * turn)
                pool.sem_inc(waits_passed, 1)
                for i in range(b * PER_TURN, b * PER_TURN + early_of(c)):
                    nc.gpsimd.indirect_dma_start(
                        row_ring[:, i, 0:D], None, x,
                        bass.IndirectOffsetOnAxis(ap=idx_ring[:, i:i + 1], axis=0)).then_inc(early_gathered[b], 16)

            for b in range(PER_TURN):
                gather_early(0, b)
            with pool.Fori(1, FULL_TURNS) as turn:
                for b in range(PER_TURN):
                    gather_early(turn, b)
            gather_early(FULL_TURNS, 0)

            last_stores = 16 * (CHUNKS // 2 + len(tiles_of(LAST)))

            def gather(j):
                nc.gpsimd.indirect_dma_start(
                    row_ring[:, j, :], None, table,
                    bass.IndirectOffsetOnAxis(ap=idx_ring[:, j:j + 1], axis=0)).then_inc(gathered[j], 16)

            def steps(turn, slots):
                for j in range(slots):
                    pool.wait_ge(table_stored[0], last_stores)
                    pool.wait_ge(idx_ready[j // RING], turn)
                    pool.wait_ge(summed[j], turn)
                    gather(j)

            pool.wait_ge(table_stored[0], last_stores)
            pool.wait_ge(table_stored[1], 16 * (CHUNKS // 2))
            for b in range(PER_TURN):
                pool.wait_ge(early_stored[b], 16 * (FULL_TURNS + (b == 0)))
            for j in range(SLOTS):
                pool.wait_ge(idx_first, 1)
                gather(j)
            with pool.Fori(1, RAW) as turn:
                steps(turn, SLOTS)
            with pool.Fori(RAW, TURNS - 1) as turn:
                steps(turn, SLOTS - 1)
            steps(TURNS - 1, SLOTS - PADDED)

            pool.wait_ge(more_totalled, 2)
            with any_extra(pool, ENGINE.Pool):
                pool.wait_ge(ex_idx_made, 1)
                for i, edges in enumerate((src, dst)):
                    nc.gpsimd.indirect_dma_start(
                        ex_int[0:EXTRA, i, :], None, edges.rearrange("(t e) -> t e", e=P),
                        bass.IndirectOffsetOnAxis(ap=ex_idx[0:EXTRA, :], axis=0)).then_inc(ex_gathered, 16)
                pool.wait_ge(ex_idx_first, 1)
                with pool.Fori(TURNS, TURNS + EXTRA_TURNS) as turn:
                    steps(turn, SLOTS)

        @block.scalar
        def _(act):
            def iteration(turn, b):
                c = PER_TURN * turn + b
                known = isinstance(turn, int)
                r = b % 2
                if not known or c < CHUNKS:
                    n = early_of(c)
                    wait_reuse(act, early_gathered[b], 16 * PER_TURN * turn)
                    nc.scalar.copy(idx_ring[:, b * PER_TURN:b * PER_TURN + n],
                                   early_cols[:, bass.ds(c * PER_TURN, n)]).then_inc(early_idx_ready, 1)
                if not known or 0 <= c - 2 < CHUNKS:
                    w = width_of(c - 2)
                    act.wait_ge(z_turned[r], uses(turn, b, 2))
                    if not known or c >= 4:
                        act.wait_ge(h_stored[r], 16 * (uses(turn, b, 2) - 1))
                        act.wait_ge(rows_summed[r], uses(turn, b, 2) - 1)
                    nc.scalar.activation(hbuf[:, r, 0:w], ps[:, r, 0:w], ACT.Relu).then_inc(h_done[r], 1)
                if not known or 0 <= c - 3 < CHUNKS:
                    d, w = c - 3, width_of(c - 3)
                    act.wait_ge(score_summed, d + 1)
                    nc.scalar.activation(dst_score[:, bass.ds(d * CHUNK, w)], ps[:, 6, 0:w], ACT.Identity,
                                         bias=b_att_all[:, 0:1]).then_inc(score_done, 1)
                if not known or 0 <= c - 2 < CHUNKS:
                    d = c - 2
                    act.wait_ge(edges_turned, d + 1)
                    for i, cols in enumerate((src_cols, dst_cols)):
                        by_column = cols[:, 0:TILES].rearrange("e (p c) -> e c p", c=COLS)
                        last = nc.scalar.copy(by_column[:, bass.ds(d, 1), :],
                                              ps[:, 7, i * P:i * P + ROWS].unsqueeze(1))
                    last.then_inc(edges_kept, 1)
                if not known or c < CHUNKS:
                    act.wait_ge(edges_loaded[b], 32 * (turn + 1))
                    wait_reuse(act, edges_turned, max(c - 1, 0) if known else c - 1)
                    nc.scalar.copy(edge_f[:, r, 0, :], edge_int[:, b, 0, :]).then_inc(src_made[r], 1)
                    n = len(tiles_of(width_of(c)))
                    act.wait_ge(mv_done[r], uses(turn, b, 2) + 1)
                    if not known or c >= 2:
                        act.wait_ge(rstd_done[r], uses(turn, b, 2))
                    nc.scalar.activation(std[:, r, 0:n], mv[:, r, 0:n, 1], ACT.Sqrt, bias=eps[:, 0:1]
                                         ).then_inc(std_done[r], 1)
                    if width_of(c) == CHUNK:
                        nc.scalar.mul(agg[:, bass.ds(c * CHUNK, CHUNK)].rearrange("p (t d) -> p t d", d=P),
                                      ones[:, :].unsqueeze(1).broadcast_to((P, TPC, P)), 0.0).then_inc(agg_zeroed, 1)
                    else:
                        for a in range(c * CHUNK, PAD, P):
                            last = nc.scalar.mul(agg[:, a:min(a + P, PAD)], ones[:, 0:min(P, PAD - a)], 0.0)
                        last.then_inc(agg_zeroed, 1)

            act.wait_ge(consts_made, 11)
            act.wait_ge(early_cols_made, 1)
            for b in range(3):
                iteration(0, b)
            act.wait_ge(table_consts, 16 * 5)
            iteration(0, 3)
            with act.Fori(1, FULL_TURNS) as turn:
                for b in range(PER_TURN):
                    iteration(turn, b)
            for b in range(PER_TURN):
                iteration(FULL_TURNS, b)
            nc.scalar.mul(dst_score[:, NODES:PAD], ones[:, 0:PAD - NODES], 0.0).then_inc(score_done, 1)

            act.wait_ge(edges_kept, COLS)
            for b in range(PER_TURN):
                act.wait_ge(early_gathered[b], 16 * (PER_TURN * FULL_TURNS + (early_of(CHUNKS - 1) if b == 0 else 0)))
            nc.scalar.copy(idx_ring[:, :], src_cols[:, 0:SLOTS]).then_inc(idx_first, 1)
            act.wait_ge(complete_made, 1)
            act.wait_ge(score_done, CHUNKS + 1)

            def gate(turn, j, start, landed, times):
                act.wait_ge(landed, 16 * times)
                if j % RING == RING - 1:
                    first = j + 1 - RING
                    nc.scalar.copy(idx_ring[:, first:j + 1], src_cols[:, bass.ds((turn + 1) * SLOTS + first, RING)]
                                   ).then_inc(idx_ready[j // RING], 1)
                wait_reuse(act, masks_ready, buffer_free(turn, j))
                nc.scalar.activation(gate_ring[:, j % RING, :], dst_score[:, bass.ds(start, P)], ACT.Sigmoid,
                                     bias=row_ring[:, j, D:ROW]).then_inc(gates_ready, 1)

            def gru_rz(c, w):
                act.wait_ge(gru_summed, c + 1)
                nc.scalar.activation(r_blk[:, 0:w], gru_sums(w)[0], ACT.Sigmoid, bias=b_rz[:, 0:1]
                                     ).then_inc(r_done, 1)
                nc.scalar.activation(z_blk[:, 0:w], gru_sums(w)[1], ACT.Sigmoid, bias=b_rz[:, 1:2]
                                     ).then_inc(z_gate_done, 1)

            def gru_n(c, w):
                act.wait_ge(u_done, c + 1)
                nc.scalar.activation(n_blk[:, 0:w], t_blk[:, 0:w], ACT.Tanh, bias=b_gates[:, 2:3]).then_inc(n_done, 1)

            blocks_through = act.alloc_register("act_blocks_through")
            act.reg_mov(blocks_through, 0)
            act.wait_ge(gates_kept, 3)

            def early_load(turn):
                wait_reuse(act, early_z_done, turn)
                act.dma_start(early_x[:, :], early_x_dram[bass.ds(turn * P, P), :]).then_inc(early_loaded, 16)

            def early_store(turn):
                act.wait_ge(early_rows_done, turn + 1)
                act.dma_start(early_rows_dram[bass.ds(turn * P, P), :], early_out[:, :]
                              ).then_inc(early_rows_stored, 16)

            def first_half(turn):
                starts = []
                complete = None if isinstance(turn, int) else complete_blocks(turn, ENGINE.Activation)
                for j in range(SLOTS):
                    if j % HALF == 0:
                        starts += window_starts(turn, j, ENGINE.Activation)
                    gate(turn, j, starts[j], gathered[j], turn + 1)
                    if j == 1 and not isinstance(turn, int):
                        early_store(turn - 1)
                    if j == 0:
                        early_load(turn)
                    if j == 8:
                        act.wait_ge(early_mv_done, turn + 1)
                        nc.scalar.activation(early_std[:, :], early_mv[:, 1:2], ACT.Sqrt, bias=eps[:, 0:1]
                                             ).then_inc(early_std_done, 1)
                    if j == 12:
                        act.wait_ge(early_turned, turn + 1)
                        nc.scalar.activation(early_h[:, :], ps[:, 4, 0:P], ACT.Relu).then_inc(early_h_done, 1)
                    if complete is not None:
                        gru_at(j, complete)

            def second_half(turn, slots):
                starts = []
                complete = None if isinstance(turn, int) else complete_blocks(turn, ENGINE.Activation)
                for j in range(slots):
                    if j % HALF == 0:
                        starts += window_starts(turn, j, ENGINE.Activation)
                    if j < SLOTS - 1:
                        gate(turn, j, starts[j], gathered[j], turn + 1)
                    else:
                        gate(turn, j, starts[j], early_rows_loaded, turn - (RAW - 1))
                    if j == 3 and slots == SLOTS:
                        act.wait_ge(summed[SLOTS - 1], turn)
                        act.dma_start(row_ring[:, SLOTS - 1, :], early_rows_dram[bass.ds((turn - RAW) * P, P), :]
                                      ).then_inc(early_rows_loaded, 16)
                    if complete is not None:
                        gru_at(j, complete)

            def gru_at(j, complete):
                if j == SLOTS // 2 - 2:
                    with act.If_lt(blocks_through, complete):
                        gru_rz(act.snap(blocks_through, min_val=0, max_val=BLOCKS - 2), P)
                if j == SLOTS // 2 + 2:
                    with act.If_lt(blocks_through, complete):
                        gru_n(act.snap(blocks_through, min_val=0, max_val=BLOCKS - 2), P)
                        act.reg_add(blocks_through, blocks_through, 1)

            first_half(0)
            with act.Fori(1, RAW) as turn:
                first_half(turn)
            early_store(RAW - 1)
            act.wait_ge(early_rows_stored, 16 * RAW)
            with act.Fori(RAW, TURNS - 1) as turn:
                second_half(turn, SLOTS)
            second_half(TURNS - 1, SLOTS - PADDED)

            with any_extra(act, ENGINE.Activation):
                act.wait_ge(prefix_made, 1)
                count_padded(act, gates_ready)
                for q in range((SLOTS - PADDED) // RING, SLOTS // RING):
                    act.sem_inc(idx_ready[q], 1)
                act.wait_ge(ex_kept, 1)
                nc.scalar.copy(idx_ring[:, :], src_cols[:, STEPS:STEPS + SLOTS]).then_inc(ex_idx_first, 1)
                act.wait_ge(ex_starts_loaded, 16)
                with act.Fori(TURNS, TURNS + EXTRA_TURNS) as turn:
                    starts = []
                    for j in range(SLOTS):
                        if j % HALF == 0:
                            starts += window_starts(turn, j, ENGINE.Activation)
                        times = turn + 1 if j < SLOTS - PADDED else turn if j < SLOTS - 1 else turn - (TURNS - RAW - 1)
                        gate(turn, j, starts[j], gathered[j], times)

            with act.If_lt(blocks_through, BLOCKS - 1):
                with act.Fori(act.snap(blocks_through, min_val=0, max_val=BLOCKS - 2), BLOCKS - 1) as c:
                    gru_rz(c, P)
                    gru_n(c, P)
            gru_rz(BLOCKS - 1, LAST_BLOCK)
            gru_n(BLOCKS - 1, LAST_BLOCK)

            act.wait_ge(bn_line, 1)
            nc.scalar.activation(bn[:, 0:1], bn_mv[:, 1:2], ACT.Sqrt, bias=eps[:, 0:1]).then_inc(bn_std, 1)
            act.wait_ge(bn_line, 5)

            def scale_step(turn, b):
                c = PER_TURN * turn + b
                w = width_of(c)
                if not isinstance(turn, int) or turn:
                    act.wait_ge(y_turned, c + (1 - PER_TURN))
                nc.scalar.activation(y_buffer(b)[:, 0:w], agg[:, bass.ds(c * CHUNK, w)], ACT.Identity,
                                     bias=bn[:, 3:4], scale=bn[:, 2:3]).then_inc(y_done, 1)

            for b in range(PER_TURN):
                scale_step(0, b)
            with act.Fori(1, FULL_TURNS) as turn:
                for b in range(PER_TURN):
                    scale_step(turn, b)
            scale_step(FULL_TURNS, 0)

        @block.vector
        def _(dve):
            line = [0]

            def link(ins):
                line[0] += 1
                ins.then_inc(dve_line, 1)
                dve.wait_ge(dve_line, line[0])

            def iteration(turn, b):
                c = PER_TURN * turn + b
                known = isinstance(turn, int)
                if not known or c < CHUNKS:
                    tiles, r = tiles_of(width_of(c)), b % 2
                    dve.wait_ge(x_loaded[b], 16 * (turn + (1 if width_of(c) == CHUNK else len(tiles))))
                    for j, n in tiles:
                        last = nc.vector.bn_stats(stats[0:n, r, j, :], xbuf[0:n, b, j, :])
                    last.then_inc(stats_done[r], 1)
                    dve.wait_ge(stats_done[r], uses(turn, b, 2) + 1)
                    dve.sem_inc(waits_passed, 1)
                    for j, n in tiles:
                        last = nc.vector.bn_aggr(mv[0:n, r, j, :], stats[0:n, r, j, :])
                    last.then_inc(mv_done[r], 1)
                if not known or 0 <= c - 1 < CHUNKS:
                    t1, b1 = back(turn, b, 1)
                    r1, tiles = b1 % 2, tiles_of(width_of(c - 1))
                    dve.wait_ge(std_done[r1], uses(t1, b1, 2) + 1)
                    nc.vector.reciprocal(rstd[:, r1, 0:len(tiles)], std[:, r1, 0:len(tiles)]
                                         ).then_inc(rstd_done[r1], 1)
                    dve.wait_ge(rstd_done[r1], uses(t1, b1, 2) + 1)
                    wait_reuse(dve, z_turned[r1], uses(t1, b1, 2))
                    dve.sem_inc(waits_passed, 1)
                    for j, n in tiles:
                        last = nc.vector.tensor_scalar(zbuf[0:n, r1, j, :], xbuf[0:n, b1, j, :],
                                                       mv[0:n, r1, j, 0:1], rstd[0:n, r1, j:j + 1],
                                                       ALU.subtract, ALU.mult)
                    last.then_inc(z_done[b1], 1)
                if not known or c < CHUNKS:
                    dve.wait_ge(edges_loaded[b], 32 * (turn + 1))
                    wait_reuse(dve, edges_turned, max(c - 1, 0) if known else c - 1)
                    dve.sem_inc(waits_passed, 1)
                    nc.vector.tensor_scalar(edge_f[:, r, 1, :], edge_int[:, b, 1, :], edge_int[:, b, 1, 0:1], None,
                                            ALU.subtract).then_inc(dst_made[r], 1)
                if not known or 0 <= c - 3 < CHUNKS:
                    t3, b3 = back(turn, b, 3)
                    d, r = c - 3, b3 % 2
                    dve.wait_ge(rows_summed[r], uses(t3, b3, 2) + 1)
                    if not known or d >= 2:
                        dve.wait_ge(table_stored[r], 16 * uses(t3, b3, 2))
                    if width_of(d) == CHUNK:
                        for half in range(2):
                            last = nc.vector.tensor_tensor(
                                rows_out[:, r, 2 * half:2 * half + 2, :],
                                ps[:, 2 + 2 * r + half, :].rearrange("p (t d) -> p t d", t=2)[:, :, 0:ROW],
                                b_table[:, :].unsqueeze(1).broadcast_to((P, 2, ROW)), ALU.add)
                    else:
                        for j, n in tiles_of(LAST):
                            last = nc.vector.tensor_tensor(rows_out[0:n, r, j, :], ps_rows(r, j)[0:n, :],
                                                           b_table[0:n, :], ALU.add)
                    last.then_inc(rows_done[r], 1)

            dve.wait_ge(consts_made, 11)
            dve.wait_ge(early_src_loaded, 16)
            nc.vector.tensor_copy(ex_f[0:WHOLE - RAW, 0, :], ex_int[0:WHOLE - RAW, 0, :]).then_inc(early_src_made, 1)
            dve.wait_ge(early_src_turned, 1)
            nc.vector.tensor_copy(early_cols[:, :], ps[:, 5, 0:RAW]).then_inc(early_cols_made, 1)
            iteration(0, 0)
            iteration(0, 1)
            dve.wait_ge(table_consts, 16 * 5)
            nc.vector.tensor_scalar(w_att_dst_wide[:, :], ones[:, :], w_att_dst[:, 0:1], None, ALU.mult
                                    ).then_inc(wide_made, 1)
            for c in range(2, 2 * PER_TURN):
                iteration(c // PER_TURN, c % PER_TURN)
            with dve.Fori(2, FULL_TURNS) as turn:
                for b in range(PER_TURN):
                    iteration(turn, b)
            for b in range(PER_TURN):
                iteration(FULL_TURNS, b)

            dve.wait_ge(firsts_loaded, 32)
            link(nc.vector.tensor_tensor(more_i[:, :], last_i[:, :], first_i[:, :], ALU.subtract))
            link(nc.vector.tensor_scalar(more_i[:, :], more_i[:, :], P.bit_length() - 1, None, ALU.arith_shift_right))
            link(nc.vector.tensor_copy(more_f[:, :], more_i[:, :]))
            nc.vector.tensor_reduce(more_row[:, :], more_f[:, :], AX_X, ALU.add).then_inc(more_counted, 1)
            dve.wait_ge(more_totalled, 1)
            nc.vector.tensor_copy(more_all[0:1, :], ps[0:1, 7, 0:1])
            link(nc.vector.tensor_scalar(none_more[0:1, :], ps[0:1, 7, 0:1], 0.5, None, ALU.is_lt))
            dve.wait_ge(starts_loaded, 16)
            ready = complete_all[:, :]
            turn_starts = starts_all[:, 0:STEPS].rearrange("o (t j) -> o t j", j=SLOTS)[:, :, 0]
            link(nc.vector.tensor_scalar(ready, turn_starts, P.bit_length() - 1, None, ALU.arith_shift_right))
            nc.vector.tensor_scalar(ready, ready, float(BLOCKS - 1), none_more[0:1, 0:1], ALU.min, ALU.mult
                                    ).then_inc(complete_made, 1)
            nc.vector.tensor_copy(row_before[0:1, :], none_more[0:1, :]).then_inc(more_totalled, 1)
            dve.wait_ge(gru_consts, 16 * 10)
            nc.vector.tensor_tensor(b_rz[:, :], b_gates[:, 0:2], b_gates[:, 3:5], ALU.add).then_inc(gates_kept, 1)
            for g in range(2):
                dve.wait_ge(gates_turned, g + 1)
                nc.vector.tensor_copy(gates[:, 3 * g:3 * g + 3, :],
                                      ps[:, 5 + g, 0:3 * P].rearrange("p (g d) -> p g d", d=P)).then_inc(gates_kept, 1)
            nc.vector.memset(bn[:, 0:4], 0.0).then_inc(block_free, 1)

            def mask(turn, j):
                dve.wait_ge(gates_ready, turn * SLOTS + (j + 1))
                k, times = earlier(turn, j, RING)
                wait_reuse(dve, summed[k], times)
                nc.vector.scalar_tensor_tensor(
                    out=mask_ring[:, j % RING, :], in0=lane[:, :], scalar=dst_cols[:, bass.ds(turn * SLOTS + j, 1)],
                    in1=gate_ring[:, j % RING, :], op0=ALU.is_equal, op1=ALU.mult).then_inc(masks_ready, 1)

            def add(turn, j, start):
                dve.wait_ge(summed[j], turn + 1)
                wait_reuse(dve, steps_added, turn * SLOTS + j)
                window = agg[:, bass.ds(start, P)]
                nc.vector.tensor_tensor(window, ps_slot(j), window, ALU.add).then_inc(steps_added, 1)

            def gru_tu(c, w):
                dve.wait_ge(r_done, c + 1)
                dve.wait_ge(z_gate_done, c + 1)
                nc.vector.scalar_tensor_tensor(out=t_blk[:, 0:w], in0=gru_sums(w)[3], scalar=b_gates[:, 5:6],
                                               in1=r_blk[:, 0:w], op0=ALU.add, op1=ALU.mult).then_inc(gru_line, 1)
                dve.wait_ge(gru_line, 4 * c + 1)
                nc.vector.tensor_tensor(t_blk[:, 0:w], gru_sums(w)[2], t_blk[:, 0:w], ALU.add
                                        ).then_inc(u_done, 1)

            def gru_new(c, w):
                dve.wait_ge(n_done, c + 1)
                dve.wait_ge(h_loaded, 16 * (c + 1))
                new = agg[:, bass.ds(c * P, w)]
                nc.vector.tensor_tensor(t_blk[:, 0:w], h_blk[:, 0:w], n_blk[:, 0:w], ALU.subtract).then_inc(gru_line, 1)
                dve.wait_ge(gru_line, 4 * c + 2)
                nc.vector.tensor_tensor(t_blk[:, 0:w], z_blk[:, 0:w], t_blk[:, 0:w], ALU.mult).then_inc(gru_line, 1)
                dve.wait_ge(gru_line, 4 * c + 3)
                nc.vector.tensor_tensor(new, n_blk[:, 0:w], t_blk[:, 0:w], ALU.add).then_inc(gru_line, 1)
                dve.wait_ge(gru_line, 4 * c + 4)
                nc.vector.bn_stats(bn_all[:, bass.ds(c, 1), :].rearrange("p o s -> p (o s)"), new
                                   ).then_inc(block_free, 1)

            blocks_through = dve.alloc_register("dve_blocks_through")
            dve.reg_mov(blocks_through, 0)
            dve.wait_ge(agg_zeroed, CHUNKS)
            dve.wait_ge(edges_kept, COLS)
            dve.wait_ge(complete_made, 1)

            def first_half(turn):
                starts = []
                complete = None if isinstance(turn, int) else complete_blocks(turn, ENGINE.DVE)
                for j in range(SLOTS):
                    if j % HALF == 0:
                        starts += window_starts(turn, j, ENGINE.DVE)
                    mask(turn, j)
                    if j >= LAG:
                        add(turn, j - LAG, starts[j - LAG])
                    if j == 4:
                        dve.wait_ge(early_loaded, 16 * (turn + 1))
                        nc.vector.bn_stats(early_stats[:, :], early_x[:, :]).then_inc(early_stats_done, 1)
                        dve.wait_ge(early_stats_done, turn + 1)
                        dve.sem_inc(waits_passed, 1)
                        nc.vector.bn_aggr(early_mv[:, :], early_stats[:, :]).then_inc(early_mv_done, 1)
                    if j == 9:
                        dve.wait_ge(early_std_done, turn + 1)
                        nc.vector.reciprocal(early_rstd[:, :], early_std[:, :]).then_inc(early_rstd_done, 1)
                        dve.wait_ge(early_rstd_done, turn + 1)
                        wait_reuse(dve, early_turned, turn)
                        dve.sem_inc(waits_passed, 1)
                        nc.vector.tensor_scalar(early_z[:, :], early_x[:, :], early_mv[:, 0:1], early_rstd[:, 0:1],
                                                ALU.subtract, ALU.mult).then_inc(early_z_done, 1)
                    if j == 15:
                        dve.wait_ge(early_summed, turn + 1)
                        wait_reuse(dve, early_rows_stored, 16 * turn)
                        nc.vector.tensor_tensor(early_out[:, :], ps[:, 5, 0:ROW], b_table[:, :], ALU.add
                                                ).then_inc(early_rows_done, 1)
                    if complete is not None:
                        gru_at(j, complete)
                for j in range(SLOTS - LAG, SLOTS):
                    add(turn, j, starts[j])

            def second_half(turn, slots):
                starts = []
                complete = None if isinstance(turn, int) else complete_blocks(turn, ENGINE.DVE)
                for j in range(slots):
                    if j % HALF == 0:
                        starts += window_starts(turn, j, ENGINE.DVE)
                    mask(turn, j)
                    if j >= LAG:
                        add(turn, j - LAG, starts[j - LAG])
                    if complete is not None:
                        gru_at(j, complete)
                for j in range(slots - LAG, slots):
                    add(turn, j, starts[j])

            def gru_at(j, complete):
                if j == SLOTS // 2:
                    with dve.If_lt(blocks_through, complete):
                        gru_tu(dve.snap(blocks_through, min_val=0, max_val=BLOCKS - 2), P)
                if j == SLOTS // 2 + 4:
                    with dve.If_lt(blocks_through, complete):
                        gru_new(dve.snap(blocks_through, min_val=0, max_val=BLOCKS - 2), P)
                        dve.reg_add(blocks_through, blocks_through, 1)

            first_half(0)
            with dve.Fori(1, RAW) as turn:
                first_half(turn)
            with dve.Fori(RAW, TURNS - 1) as turn:
                second_half(turn, SLOTS)
            second_half(TURNS - 1, SLOTS - PADDED)

            with any_extra(dve, ENGINE.DVE):
                count_padded(dve, masks_ready, steps_added)
                nc.vector.tensor_tensor_scan(more_sum[:, :], ones[0:ROWS, 0:COLS], more_f[:, :], 0.0, ALU.mult, ALU.add
                                             ).then_inc(prefix_made, 1)
                dve.wait_ge(prefix_summed, 1)
                link(nc.vector.tensor_copy(row_before[:, :], ps[0:ROWS, 7, 0:1]))
                link(nc.vector.tensor_scalar(more_sum[:, :], more_sum[:, :], row_before[:, 0:1], None, ALU.add))
                link(nc.vector.memset(count[:, :, :], 0.0))
                for c in range(COLS):
                    link(nc.vector.tensor_scalar(at_or_below[:, :], lane[0:ROWS, 0:EXTRA], more_sum[:, c:c + 1], None,
                                                 ALU.is_ge))
                    nc.vector.tensor_tensor(count[:, 0, :], count[:, 0, :], at_or_below[:, :], ALU.add)
                    link(nc.vector.scalar_tensor_tensor(
                        out=count[:, 1, :], in0=at_or_below[:, :], scalar=more_f[:, c:c + 1], in1=count[:, 1, :],
                        op0=ALU.mult, op1=ALU.add))
                nc.vector.tensor_copy(row_before[:, :], count[:, 0, 0:1]).then_inc(ex_counted, 1)
                dve.wait_ge(ex_counts_summed, 1)
                tile_k, done_k = ps[0:EXTRA, 7, 8:9], ps[0:EXTRA, 7, 16:17]
                e = ex[0:EXTRA, :]
                nc.vector.tensor_scalar(ex_idx[0:EXTRA, :], tile_k, float(TILES - 1), None, ALU.min
                                        ).then_inc(ex_idx_made, 1)
                nc.vector.tensor_scalar(e[:, 0:1], tile_k, float(TILES), None, ALU.is_ge)
                link(nc.vector.tensor_tensor(e[:, 1:2], lane_p[0:EXTRA, :], done_k, ALU.subtract))
                link(nc.vector.tensor_scalar(e[:, 1:2], e[:, 1:2], 1.0, float(P), ALU.add, ALU.mult))
                dve.wait_ge(ex_gathered, 32)
                link(nc.vector.tensor_copy(ex_f[0:EXTRA, :, :], ex_int[0:EXTRA, :, :]))
                link(nc.vector.tensor_tensor(e[:, 2:3], e[:, 1:2], ex_f[0:EXTRA, 1, 0:1], ALU.add))
                link(nc.vector.tensor_scalar(e[:, 3:4], e[:, 2:3], -1.0, float(NODES), ALU.mult, ALU.add))
                link(nc.vector.tensor_tensor(e[:, 4:5], e[:, 3:4], e[:, 0:1], ALU.mult))
                link(nc.vector.tensor_tensor(e[:, 5:6], e[:, 4:5], e[:, 2:3], ALU.add))
                link(nc.vector.tensor_copy(ex_start[0:EXTRA, :], e[:, 5:6]))
                nc.vector.tensor_scalar(ex_f[0:EXTRA, 1, :], ex_f[0:EXTRA, 1, :], e[:, 5:6], None, ALU.subtract
                                        ).then_inc(ex_made, 1)
                dve.wait_ge(ex_turned, 1)
                nc.vector.tensor_copy(src_cols[:, STEPS:STEPS + EXTRA], ps[:, 6, 0:EXTRA])
                nc.vector.tensor_copy(dst_cols[:, STEPS:STEPS + EXTRA], ps[:, 6, P:P + EXTRA]).then_inc(ex_kept, 1)
                dve.wait_ge(ex_starts_loaded, 16)
                dve.wait_ge(ex_kept, 1)
                with dve.Fori(TURNS, TURNS + EXTRA_TURNS) as turn:
                    starts = []
                    for j in range(SLOTS):
                        if j % HALF == 0:
                            starts += window_starts(turn, j, ENGINE.DVE)
                        mask(turn, j)
                        add(turn, j, starts[j])

            nc.vector.memset(bn[:, 0:4], 0.0).then_inc(agg_complete, 1)
            with dve.If_lt(blocks_through, BLOCKS - 1):
                with dve.Fori(dve.snap(blocks_through, min_val=0, max_val=BLOCKS - 2), BLOCKS - 1) as c:
                    gru_tu(c, P)
                    gru_new(c, P)
            gru_tu(BLOCKS - 1, LAST_BLOCK)
            gru_new(BLOCKS - 1, LAST_BLOCK)

            dve.wait_ge(block_free, BLOCKS + 1)
            nc.vector.bn_aggr(bn_mv[:, :], bn_all[:, :, :].rearrange("p c s -> p (c s)")).then_inc(bn_line, 1)
            dve.wait_ge(bn_std, 1)
            nc.vector.reciprocal(bn[:, 1:2], bn[:, 0:1]).then_inc(bn_line, 1)
            dve.wait_ge(bn_line, 2)
            nc.vector.tensor_tensor(bn[:, 2:3], bn[:, 1:2], gamma_c[:, :], ALU.mult).then_inc(bn_line, 1)
            dve.wait_ge(bn_line, 3)
            nc.vector.tensor_tensor(bn[:, 3:4], bn_mv[:, 0:1], bn[:, 2:3], ALU.mult).then_inc(bn_line, 1)
            dve.wait_ge(bn_line, 4)
            nc.vector.tensor_tensor(bn[:, 3:4], beta_c[:, :], bn[:, 3:4], ALU.subtract).then_inc(bn_line, 1)

            def out_step(turn, b):
                c, r = PER_TURN * turn + b, b
                dve.wait_ge(y_turned, c + 1)
                wait_reuse(dve, o_stored[b], 16 * turn)
                if width_of(c) == CHUNK:
                    last = nc.vector.tensor_tensor(xbuf[:, b, :, :], ps[:, r, :].rearrange("p (t d) -> p t d", d=D),
                                                   x_again[:, bass.ds(c * TPC, TPC), :], ALU.add)
                else:
                    for j, n in tiles_of(LAST):
                        last = nc.vector.tensor_tensor(xbuf[0:n, b, j, :], ps[0:n, r, j * P:(j + 1) * P],
                                                       x_again[0:n, c * TPC + j, :], ALU.add)
                last.then_inc(o_done[b], 1)

            dve.wait_ge(x_back, 16 * X_TILES)
            for b in range(PER_TURN):
                out_step(0, b)
            with dve.Fori(1, FULL_TURNS) as turn:
                for b in range(PER_TURN):
                    out_step(turn, b)
            out_step(FULL_TURNS, 0)

        @block.tensor
        def _(pe):
            def iteration(turn, b):
                c = PER_TURN * turn + b
                known = isinstance(turn, int)
                t1, b1 = back(turn, b, 1)
                t2, b2 = back(turn, b, 2)
                if not known or 0 <= c - 1 < CHUNKS:
                    r1 = b1 % 2
                    pe.wait_ge(z_done[b1], t1 + 1)
                    wait_reuse(pe, h_done[r1], uses(t1, b1, 2))
                    for j, n in tiles_of(width_of(c - 1)):
                        last = nc.tensor.transpose(ps[:, r1, j * P:j * P + n], zbuf[0:n, r1, j, :], ident[0:n, 0:n])
                    last.then_inc(z_turned[r1], 1)
                if not known or 0 <= c - 2 < CHUNKS:
                    r2, w = b2 % 2, width_of(c - 2)
                    pe.wait_ge(h_done[r2], uses(t2, b2, 2) + 1)
                    wait_reuse(pe, score_done, c - 2)
                    nc.tensor.matmul(ps[:, 6, 0:w], w_att_dst_wide[:, :], hbuf[:, r2, 0:w],
                                     start=True, stop=True).then_inc(score_summed, 1)
                if not known or 0 <= c - 1 < CHUNKS:
                    pe.wait_ge(src_made[r1], uses(t1, b1, 2) + 1)
                    pe.wait_ge(dst_made[r1], uses(t1, b1, 2) + 1)
                    wait_reuse(pe, edges_kept, c - 1)
                    for i in range(2):
                        last = nc.tensor.transpose(ps[:, 7, i * P:i * P + ROWS], edge_f[:, r1, i, :],
                                                   ident[0:ROWS, 0:ROWS])
                    last.then_inc(edges_turned, 1)
                if not known or 0 <= c - 2 < CHUNKS:
                    wait_reuse(pe, rows_done[r2], uses(t2, b2, 2))
                    for j, n in tiles_of(w):
                        last = nc.tensor.matmul(ps_rows(r2, j)[0:n, :], hbuf[:, r2, j * P:j * P + n], w_table[:, :],
                                                start=True, stop=True)
                    last.then_inc(rows_summed[r2], 1)

            pe.wait_ge(consts_made, 11)
            pe.wait_ge(early_src_made, 1)
            nc.tensor.transpose(ps[:, 5, 0:RAW], ex_f[0:RAW, 0, :], ident[0:RAW, 0:RAW]).then_inc(early_src_turned, 1)
            iteration(0, 0)
            iteration(0, 1)
            pe.wait_ge(wide_made, 1)
            pe.wait_ge(early_cols_made, 1)
            for b in range(2, PER_TURN):
                iteration(0, b)
            with pe.Fori(1, FULL_TURNS) as turn:
                for b in range(PER_TURN):
                    iteration(turn, b)
            for b in range(3):
                iteration(FULL_TURNS, b)
            pe.wait_ge(edges_kept, COLS)
            pe.wait_ge(score_done, CHUNKS)
            pe.wait_ge(rows_done[0], CHUNKS // 2 + 1)
            pe.wait_ge(rows_done[1], CHUNKS // 2)
            pe.wait_ge(more_counted, 1)
            nc.tensor.matmul(ps[:, 7, 0:1], ones[0:ROWS, :], more_row[:, :], start=True, stop=True
                             ).then_inc(more_totalled, 1)
            pe.wait_ge(gru_consts, 16 * 10)
            for g in range(2):
                for i in range(3):
                    last = nc.tensor.transpose(ps[:, 5 + g, i * P:(i + 1) * P], gates_nat[:, 3 * g + i, :], ident[:, :])
                last.then_inc(gates_turned, 1)
            pe.wait_ge(gates_kept, 3)
            pe.wait_ge(more_totalled, 2)
            pe.wait_ge(complete_made, 1)

            def scatter(turn, j):
                pe.wait_ge(masks_ready, turn * SLOTS + (j + 1))
                wait_reuse(pe, steps_added, buffer_free(turn, j))
                nc.tensor.matmul(ps_slot(j), row_ring[:, j, 0:D], mask_ring[:, j % RING, :],
                                 start=True, stop=True).then_inc(summed[j], 1)

            def gru(c, w):
                pe.wait_ge(h_loaded, 16 * (c + 1))
                pe.wait_ge(block_free, c + 1)
                a, h = agg[:, bass.ds(c * P, w)], h_blk[:, 0:w]
                *rz_sums, i_n, h_n = gru_sums(w)
                for g, total in enumerate(rz_sums):
                    nc.tensor.matmul(total, gates[:, 3 + g, :], h, start=True, stop=False)
                    nc.tensor.matmul(total, gates[:, g, :], a, start=False, stop=True)
                nc.tensor.matmul(h_n, gates[:, 5, :], h, start=True, stop=True)
                nc.tensor.matmul(i_n, gates[:, 2, :], a, start=True, stop=True
                                 ).then_inc(gru_summed, 1)

            blocks_through = pe.alloc_register("pe_blocks_through")
            pe.reg_mov(blocks_through, 0)

            def gru_in_turn(turn, complete):
                with pe.If_lt(blocks_through, complete):
                    pe.wait_ge(steps_added, turn * SLOTS)
                    gru(pe.snap(blocks_through, min_val=0, max_val=BLOCKS - 2), P)
                    pe.reg_add(blocks_through, blocks_through, 1)

            def first_half(turn):
                complete = None if isinstance(turn, int) else complete_blocks(turn, ENGINE.PE)
                for j in range(SLOTS):
                    scatter(turn, j)
                    if j == 1 and complete is not None:
                        gru_in_turn(turn, complete)
                    if j == 10:
                        pe.wait_ge(early_z_done, turn + 1)
                        wait_reuse(pe, early_h_done, turn)
                        nc.tensor.transpose(ps[:, 4, 0:P], early_z[:, :], ident[:, :]).then_inc(early_turned, 1)
                    if j == 13:
                        pe.wait_ge(early_h_done, turn + 1)
                        wait_reuse(pe, early_rows_done, turn)
                        nc.tensor.matmul(ps[:, 5, 0:ROW], early_h[:, :], w_table[:, :], start=True, stop=True
                                         ).then_inc(early_summed, 1)

            first_half(0)
            with pe.Fori(1, RAW) as turn:
                first_half(turn)
            with pe.Fori(RAW, TURNS - 1) as turn:
                complete = complete_blocks(turn, ENGINE.PE)
                for j in range(SLOTS):
                    scatter(turn, j)
                    if j == 1:
                        gru_in_turn(turn, complete)
            for j in range(SLOTS - PADDED):
                scatter(TURNS - 1, j)

            with any_extra(pe, ENGINE.PE):
                pe.wait_ge(prefix_made, 1)
                for j in range(SLOTS - PADDED, SLOTS):
                    pe.sem_inc(summed[j], 1)
                nc.tensor.matmul(ps[0:ROWS, 7, 0:1], before[0:ROWS, 0:ROWS], more_sum[:, COLS - 1:COLS],
                                 start=True, stop=True).then_inc(prefix_summed, 1)
                pe.wait_ge(ex_counted, 1)
                nc.tensor.matmul(ps[0:EXTRA, 7, 8:9], count[:, 0, :], ones[0:ROWS, 0:1], start=True, stop=True)
                nc.tensor.matmul(ps[0:EXTRA, 7, 16:17], count[:, 1, :], ones[0:ROWS, 0:1], start=True, stop=True
                                 ).then_inc(ex_counts_summed, 1)
                pe.wait_ge(ex_made, 1)
                for i in range(2):
                    last = nc.tensor.transpose(ps[:, 6, i * P:i * P + EXTRA], ex_f[0:EXTRA, i, :],
                                               ident[0:EXTRA, 0:EXTRA])
                last.then_inc(ex_turned, 1)
                with pe.Fori(TURNS, TURNS + EXTRA_TURNS) as turn:
                    for j in range(SLOTS):
                        scatter(turn, j)

            pe.wait_ge(agg_complete, 1)
            with pe.If_lt(blocks_through, BLOCKS - 1):
                with pe.Fori(pe.snap(blocks_through, min_val=0, max_val=BLOCKS - 2), BLOCKS - 1) as c:
                    gru(c, P)
            gru(BLOCKS - 1, LAST_BLOCK)

            def back_step(turn, b):
                c = PER_TURN * turn + b
                pe.wait_ge(y_done, c + 1)
                wait_reuse(pe, o_done[b], turn)
                for j, n in tiles_of(width_of(c)):
                    last = nc.tensor.transpose(ps[0:n, b, j * P:(j + 1) * P], y_buffer(b)[:, j * P:j * P + n],
                                               ident[:, :])
                last.then_inc(y_turned, 1)

            for b in range(PER_TURN):
                back_step(0, b)
            with pe.Fori(1, FULL_TURNS) as turn:
                for b in range(PER_TURN):
                    back_step(turn, b)
            back_step(FULL_TURNS, 0)


_INS = ['x', 'src', 'dst', 'L0_gnn_W_msg', 'L0_gnn_b_msg', 'L0_gnn_W_att', 'L0_gnn_b_att', 'L0_gnn_W_ih',
        'L0_gnn_b_ih', 'L0_gnn_W_hh', 'L0_gnn_b_hh', 'L0_gnn_gamma', 'L0_gnn_beta']


def kernel(**inputs):
    import numpy as _np
    import concourse.bacc as _bacc
    from concourse import mybir as _mybir
    from concourse.bass_utils import run_bass_kernel_spmd as _run

    nc = _bacc.Bacc("TRN2", target_bir_lowering=False, num_devices=1)
    arrays, args = {}, []
    for name in _INS:
        a = _np.ascontiguousarray(inputs[name])
        arrays[f"in_{name}_dram"] = a
        args.append(nc.dram_tensor(f"in_{name}_dram", a.shape, _mybir.dt.from_np(a.dtype), kind="ExternalInput").ap())
    shape = inputs['x'].shape
    args.append(nc.dram_tensor("out_0_dram", shape, _mybir.dt.float32, kind="ExternalOutput").ap())
    gnn_program(nc, *args)
    r = _run(nc, [arrays], core_ids=[0])
    return r.results[0]["out_0_dram"]
```
